# Optimizing a Trainium2 kernel written in Bass

```python
import numpy as np
import jax
import jax.numpy as jnp

def _softmax(x, axis=-1):
    return jax.nn.softmax(x, axis=axis)

def _gelu(x):
    return jax.nn.gelu(x, approximate=True)

def _silu(x):
    return jax.nn.silu(x)

def _sigmoid(x):
    return jax.nn.sigmoid(x)

def _layernorm(x, axis=-1, eps=1e-05):
    m = jnp.mean(x, axis=axis, keepdims=True)
    v = jnp.var(x, axis=axis, keepdims=True)
    return (x - m) / jnp.sqrt(v + eps)

def _scatter_add(tgt, idx, src, axis=0):
    return tgt.at[idx].add(src)

def _segment_sum(src, seg, n):
    return jax.ops.segment_sum(src, seg, n)
kernel_name = 'mk_adaln_ffn_d1_seqx_r4_c4f3bc'

def setup_inputs(seed: int=0):
    np.random.seed(seed)
    _w = jnp.asarray

    def _rec_inputs():
        import jax
        import jax.numpy as jnp
        _rk = jax.random.key(seed)
        x = -1.394e-06 + 0.9999 * jax.random.normal(jax.random.fold_in(_rk, 1), (8, 256, 512), jnp.float32)
        _lenS = 256 - jax.random.randint(jax.random.fold_in(_rk, 7), (8,), 0, max(1, 256 // 4) + 1, jnp.int32)
        _lenS2 = 256 - jax.random.randint(jax.random.fold_in(_rk, 8), (8,), 0, max(1, 256 // 4) + 1, jnp.int32)
        cond_2048 = -0.00499425 + 1.0058 * jax.random.normal(jax.random.fold_in(_rk, 11), (8, 512), jnp.float32)
        return (x, cond_2048)
    x, cond_2048 = _rec_inputs()

    def _L0_cond_setup():
        import jax, jax.numpy as jnp
        import numpy as np
        B, T, D = (16, 128, 512)
        key = jax.random.key(seed)
        k0, k1, k2, k3 = jax.random.split(key, 4)
        scale = 1.0 / np.sqrt(D)
        return {'initial_state': jax.random.normal(k0, (B, D), jnp.float32), 'inputs': jax.random.normal(k1, (B, T, D), jnp.float32), 'W_ih': jax.random.normal(k2, (D, 3 * D), jnp.float32) * scale, 'W_hh': jax.random.normal(k3, (D, 3 * D), jnp.float32) * scale, 'b_ih': jnp.zeros((3 * D,), jnp.float32), 'b_hh': jnp.zeros((3 * D,), jnp.float32)}
    _L0_cond_all = _L0_cond_setup()
    _L0_cond_in = {k: v for k, v in _L0_cond_all.items() if k in ('W_ih', 'W_hh', 'b_ih', 'b_hh')}
    del _L0_cond_all

    def _L0_ffn_setup():
        import jax, jax.numpy as jnp
        import numpy as np
        H = 512
        E = 8
        TOPK = 2
        I_MOE = 256
        I_SH = 1024

        def _silu_and_mul(gu):
            g, u = jnp.split(gu, 2, axis=-1)
            return jax.nn.silu(g) * u
        key = jax.random.key(seed)
        ks = jax.random.split(key, 6)
        s = lambda *sh: 1.0 / np.sqrt(sh[-2])
        hidden_states = jax.random.normal(ks[0], (2, 256, H), dtype=jnp.float32)
        w_gate = jax.random.normal(ks[1], (H, E), dtype=jnp.float32) * (1.0 / np.sqrt(H))
        w_gate_up = jax.random.normal(ks[2], (E, H, 2 * I_MOE), dtype=jnp.float32) * (1.0 / np.sqrt(H))
        w_down = jax.random.normal(ks[3], (E, I_MOE, H), dtype=jnp.float32) * (1.0 / np.sqrt(I_MOE))
        w_sh_gate_up = jax.random.normal(ks[4], (H, 2 * I_SH), dtype=jnp.float32) * (1.0 / np.sqrt(H))
        w_sh_down = jax.random.normal(ks[5], (I_SH, H), dtype=jnp.float32) * (1.0 / np.sqrt(I_SH))
        return {'hidden_states': hidden_states, 'w_gate': w_gate, 'w_gate_up': w_gate_up, 'w_down': w_down, 'w_sh_gate_up': w_sh_gate_up, 'w_sh_down': w_sh_down}
    _L0_ffn_all = _L0_ffn_setup()
    _L0_ffn_in = {k: v for k, v in _L0_ffn_all.items() if k in ('w_gate', 'w_gate_up', 'w_down', 'w_sh_gate_up', 'w_sh_down')}
    del _L0_ffn_all
    return {'x': x, 'cond_2048': cond_2048, 'L0_cond_W_ih': _L0_cond_in['W_ih'], 'L0_cond_W_hh': _L0_cond_in['W_hh'], 'L0_cond_b_ih': _L0_cond_in['b_ih'], 'L0_cond_b_hh': _L0_cond_in['b_hh'], 'L0_ffn_w_gate': _L0_ffn_in['w_gate'], 'L0_ffn_w_gate_up': _L0_ffn_in['w_gate_up'], 'L0_ffn_w_down': _L0_ffn_in['w_down'], 'L0_ffn_w_sh_gate_up': _L0_ffn_in['w_sh_gate_up'], 'L0_ffn_w_sh_down': _L0_ffn_in['w_sh_down']}

def reference(x, cond_2048, L0_cond_W_ih, L0_cond_W_hh, L0_cond_b_ih, L0_cond_b_hh, L0_ffn_w_gate, L0_ffn_w_gate_up, L0_ffn_w_down, L0_ffn_w_sh_gate_up, L0_ffn_w_sh_down):
    import jax
    import jax.numpy as jnp

    def _L0_cond_ref(initial_state, inputs, W_ih, W_hh, b_ih, b_hh):
        import jax, jax.numpy as jnp
        import numpy as np
        B, T, D = (16, 128, 512)
        "ScanOverTime(GRU cell): sequential per-timestep module call with\n            dict-state passing; merge_dict_trees stacks the per-step\n            'state_predicted' tensors along axis=1 -> [B, T, D]."

        def cell(h, x):
            gi = x @ W_ih + b_ih
            gh = h @ W_hh + b_hh
            i_r, i_z, i_n = jnp.split(gi, 3, axis=-1)
            h_r, h_z, h_n = jnp.split(gh, 3, axis=-1)
            r = jax.nn.sigmoid(i_r + h_r)
            z = jax.nn.sigmoid(i_z + h_z)
            n = jnp.tanh(i_n + r * h_n)
            h_new = (1.0 - z) * n + z * h
            return (h_new, h_new)
        xs = jnp.swapaxes(inputs, 0, 1)
        _, hs = jax.lax.scan(cell, initial_state, xs)
        return jnp.swapaxes(hs, 0, 1)

    def _L0_ffn_ref(hidden_states, w_gate, w_gate_up, w_down, w_sh_gate_up, w_sh_down):
        import jax, jax.numpy as jnp
        import numpy as np
        H = 512
        E = 8
        TOPK = 2
        I_MOE = 256
        I_SH = 1024

        def _silu_and_mul(gu):
            g, u = jnp.split(gu, 2, axis=-1)
            return jax.nn.silu(g) * u
        orig_shape = hidden_states.shape
        x = hidden_states.reshape(-1, orig_shape[-1])
        router_logits = x @ w_gate
        probs = jax.nn.softmax(router_logits, axis=-1)
        topk_w, topk_ids = jax.lax.top_k(probs, TOPK)
        topk_w = topk_w / jnp.sum(topk_w, axis=-1, keepdims=True)
        combine = jnp.sum(topk_w[..., None] * jax.nn.one_hot(topk_ids, E, dtype=x.dtype), axis=1)
        gu = jnp.einsum('th,ehf->etf', x, w_gate_up)
        act = _silu_and_mul(gu)
        eo = jnp.einsum('eti,eih->eth', act, w_down)
        routed = jnp.einsum('te,eth->th', combine, eo)
        shared = _silu_and_mul(x @ w_sh_gate_up) @ w_sh_down
        return (routed + shared).reshape(orig_shape)
    x = x + _L0_ffn_ref(_L0_cond_ref(cond_2048, x, L0_cond_W_ih, L0_cond_W_hh, L0_cond_b_ih, L0_cond_b_hh), L0_ffn_w_gate, L0_ffn_w_gate_up, L0_ffn_w_down, L0_ffn_w_sh_gate_up, L0_ffn_w_sh_down)
    return x

_drawn_inputs = setup_inputs


def setup_inputs(seed=0):
    import zlib

    import numpy as np

    out = dict(_drawn_inputs(seed))
    spreads = {'L0_cond_b_ih': (0.0, 0.1), 'L0_cond_b_hh': (0.0, 0.339)}
    factors = {}
    for name, (base, spread) in spreads.items():
        noise = np.random.default_rng([zlib.crc32(name.encode()), seed]).standard_normal(out[name].shape)
        drawn = base * np.exp(spread * noise) if base else spread * noise
        out[name] = jnp.asarray(drawn.astype(out[name].dtype))
    for name, factor in factors.items():
        out[name] = (out[name] * factor).astype(out[name].dtype)
    return out
```

```python
from contextlib import ExitStack

import numpy as np

import concourse.bass as bass
from concourse import mybir

ALU = mybir.AluOpType
ACT = mybir.ActivationFunctionType
AX = mybir.AxisListType
F32 = mybir.dt.float32
F16 = mybir.dt.float16
U32 = mybir.dt.uint32
U8 = mybir.dt.uint8

P = 128
B, T, D = 8, 256, 512
KC = 4
E = 8
TB = 32
NBLK = T // TB
N = TB * B
SUB = 16
CH = 2048
NCHUNK = 24
A_SH = 2.0 ** -64
A_RT = 2.0 ** -74
CB = 1024.0
QUOTA = 3100.0


class Flow:

    def __init__(self, nc, ctx):
        self.nc, self.ctx = nc, ctx
        self.q = {k: [] for k in ("pe", "dve", "act", "sp")}
        self.count = {}
        self.sems = {}

    def sem(self, name):
        self.sems[name] = self.ctx.enter_context(self.nc.semaphore(name))
        self.count[name] = 0
        return name

    def op(self, eng, fn, waits=(), post=None, by=1):
        if post is not None:
            self.count[post] += by
        self.q[eng].append((tuple(w for w in waits if w is not None), fn, post, by))
        return (post, self.count[post]) if post is not None else None

    def play(self, eng, e):
        met = {}
        for waits, fn, post, by in self.q[eng]:
            need = {}
            for s, v in waits:
                need[s] = max(need.get(s, 0), v)
            for s, v in need.items():
                if met.get(s, 0) < v:
                    e.wait_ge(self.sems[s], v)
                    met[s] = v
            ins = fn(e)
            if post is not None:
                ins.then_inc(self.sems[post], by)


def adaln_ffn(nc, x, h0, wih, whh, bih, bhh, wr, wgu, wd, ident, iota, y):
    with ExitStack() as ctx:
        f = Flow(nc, ctx)

        def psum(name):
            return ctx.enter_context(nc.psum_tensor(name, [P, 512], F32))

        arena = ctx.enter_context(nc.sbuf_tensor("arena", [P, 212800], U8))
        gi_d = nc.dram_tensor("gi_scratch", [NBLK // 2, P, 12, 512], F32)

        def view(off, n, dt):
            size = 2 if dt == F16 else 4
            return arena[:, off:off + n * size].bitcast(dt)

        psG = psum("psG")
        psM = psum("psM")
        psU = [psum("psU0"), psum("psU1")]
        psD = [psum(f"psD{i}") for i in range(4)]

        W_HH, W_GU, W_D = 0, 12, 60
        XR = 63
        EV = 83
        U0 = 87 * CH

        def raw(slot, n):
            return view(slot * CH, n * 512, F32)

        def half(slot, part):
            return view(slot * CH + part * 1024, 512, F16)

        W_IH_OFF = U0
        hb = [view(U0 + 4096 * k, 2048, F16).rearrange("p (s c n) -> p s c n", s=2, c=KC) for k in range(2)]
        gi = [view(U0 + 8192 + 6144 * k, 1536, F32).rearrange("p (f n) -> p f n", f=12) for k in range(2)]
        xy = view(U0 + 20480, 1024, F32).rearrange("p (c n) -> p c n", c=KC)
        X = [view(U0 + 24576 + 1024 * k, 256, F32) for k in range(2)]
        AH = [view(U0 + 26624 + 1024 * k, 512, F16).rearrange("p (s n) -> p s n", s=2) for k in range(2)]
        g0 = U0 + 28672
        Tt = view(g0, 384, F32).rearrange("p (f m) -> p f m", f=12)
        g0 += 1536
        Hs, zh, mm, qq, ww, nn, zc = [view(g0 + 128 * k, 32, F32) for k in range(7)]
        g0 += 896
        c0 = U0 + 31104
        idf = view(c0, 128, F32)
        idh = view(c0 + 512, 128, F16)
        sc = view(c0 + 768, 48, F32)
        iot = view(c0 + 960, 8, F32)
        bi = view(c0 + 992, 12, F32)
        bh = view(c0 + 1040, 12, F32)
        bs = view(c0 + 1088, 12, F32)
        bhn = view(c0 + 1136, 32, F32)
        wr_raw = view(c0 + 1264, 32, F32)
        wr_h = view(c0 + 1392, 64, F16).rearrange("p (s n) -> p s n", s=2)
        h0f = view(c0 + 1520, 32, F32)
        hst = [view(c0 + 1648 + 1728 * k, 64, F16).rearrange("p (c s n) -> p c s n", s=2, c=KC) for k in range(2)]
        mx = view(c0 + 1776, 96, F32)
        gcol = view(c0 + 2160, 16, F32)
        rt = view(c0 + 2224, 160, F32)
        cmb = view(c0 + 2864, 32, F16).rearrange("p (t s e) -> p t s e", t=2, s=2)
        idx = view(c0 + 2928, 16, U32)
        Uv = view(c0 + 2992, 64, F32)
        Un = view(c0 + 3248, 32, F32)
        assert c0 + 3504 <= 212800 and g0 <= c0

        for n_ in ("ld_a", "ld_x", "ld_ih", "ld_hh", "ld_gu", "ld_d", "ld_gi0", "ld_gi1", "ld_xy",
                   "st_gi0", "st_gi1", "st_gi2", "st_gi3", "st_y", "prep_v", "prep_a", "prep_p", "gi_p", "gi_a",
                   "gru_p", "gru_v", "gru_a", "ffn_p", "ffn_v", "ffn_a"):
            f.sem(n_)

        def ld(out, in_, post, waits=()):
            return f.op("sp", lambda e: e.dma_start(out, in_), waits, post, 16)

        def pv(fn, *waits):
            return f.op("dve", fn, waits, "prep_v")

        def pa(fn, *waits):
            return f.op("act", fn, waits, "prep_a")

        def col(k):
            return sc[:, k:k + 1]

        (PX, PIH, PHH, PH, PR, PGU, PD) = range(7)
        SX, SIH, SHH, SH_, SR, SGU, SD = range(8, 15)
        (C_SH, C_TR, C_TN, C_GI, C_C1, C_MC1, C_IR, C_MIR, C_TG, C_OUT, C_T0, C_T1) = range(16, 28)

        for out, src in ((idf, ident), (iot, iota), (bi, bih), (bh, bhh), (wr_raw, wr), (h0f, h0)):
            v_a = ld(out, src, "ld_a")
        x_slot = XR + 4
        v_x = []
        for q in range(4):
            v_x = ld(raw(x_slot + 4 * q, 4), x[:, 2048 * q:2048 * (q + 1)], "ld_x")
        ih_raw = view(W_IH_OFF + 3 * CH, 12 * 512, F32)
        v_ih = ld(ih_raw, wih, "ld_ih")
        v_hh = ld(raw(W_HH + 3, 12), whh, "ld_hh")
        for q in range(4):
            v_gu = ld(raw(W_GU + 3 + 12 * q, 12), wgu[:, 6144 * q:6144 * (q + 1)], "ld_gu")

        def rowmax(out, in_, *waits):
            return pv(lambda e: e.tensor_reduce(out, in_, AX.X, ALU.max, apply_absolute_value=True), *waits)

        def spread(k0, nk, dep):
            v = f.op("pe", lambda e: e.matmul(psM[0:nk, 0:128], gcol[:, k0:k0 + nk], idf[:, :], start=True, stop=True),
                     (dep, v_a), "prep_p")
            v = pv(lambda e: e.tensor_reduce(mx[0:nk, 64:65], psM[0:nk, 0:128], AX.X, ALU.max), v)
            v = f.op("pe", lambda e: e.matmul(psM[:, 0:nk], mx[0:nk, 64:65].broadcast_to([nk, 128]), idf[0:nk, 0:nk],
                                                start=True, stop=True), (v,), "prep_p")
            v = pv(lambda e: e.tensor_scalar(col_s(k0, nk), psM[:, 0:nk], 2.0 ** -40, None, ALU.max), v)
            return v

        def col_s(k0, nk):
            return sc[:, k0:k0 + nk]

        def floors(k0, nk, v):
            bits = sc[:, k0:k0 + nk].bitcast(U32)
            v = pv(lambda e: e.tensor_scalar(bits, bits, 0x7F800000, None, ALU.bitwise_and), v)
            v = pv(lambda e: e.reciprocal(sc[:, 8 + k0:8 + k0 + nk], sc[:, k0:k0 + nk]), v)
            return pv(lambda e: e.tensor_scalar(sc[:, 8 + k0:8 + k0 + nk], sc[:, 8 + k0:8 + k0 + nk],
                                                2.0 ** 14, None, ALU.mult), v)

        def prod(out, a, b, k, v):
            return pv(lambda e: e.scalar_tensor_tensor(out=col(out), in0=col(a), scalar=k, in1=col(b),
                                                       op0=ALU.mult, op1=ALU.mult), v)

        v_psg = pv(lambda e: e.memset(psG[:, :], 0.0))
        v_idh = pv(lambda e: e.tensor_copy(idh, idf), v_a)
        rowmax(gcol[:, PR:PR + 1], wr_raw, v_a)
        rowmax(gcol[:, PH:PH + 1], h0f, v_a)
        rowmax(gcol[:, PX:PX + 1], raw(x_slot, 16), v_x)
        rowmax(gcol[:, PIH:PIH + 1], ih_raw, v_ih)
        v = rowmax(gcol[:, PHH:PHH + 1], raw(W_HH + 3, 12), v_hh)
        v = spread(0, 5, v)
        v = pv(lambda e: e.tensor_scalar(col(PH), col(PH), 1.0, None, ALU.max), v)
        v_sc = v = floors(0, 5, v)
        v = prod(C_SH, SHH, SH_, 1.0, v)
        v = prod(C_TN, PHH, PH, 2.0 ** -28, v)
        v = pv(lambda e: e.tensor_scalar(col(C_TR), col(C_TN), 0.5, None, ALU.mult), v)
        v = prod(C_T0, PX, PIH, 2.0 ** -28, v)
        v = prod(C_GI, C_T0, C_SH, 1.0, v)
        v = pv(lambda e: e.tensor_scalar(col(C_C1), col(SH_), 0.5, None, ALU.mult), v)
        v = pv(lambda e: e.tensor_scalar(col(C_MC1), col(SH_), -0.5, None, ALU.mult), v)
        v = prod(C_IR, PR, PH, 2.0 ** -28, v)
        v = prod(C_MIR, PR, PH, -(2.0 ** -28), v)
        v = pv(lambda e: e.tensor_tensor(bs[:, 0:8], bi[:, 0:8], bh[:, 0:8], ALU.add), v)
        v = pv(lambda e: e.tensor_copy(bs[:, 8:12], bi[:, 8:12]), v)
        v = pv(lambda e: e.tensor_scalar(bs, bs, col(C_SH), None, ALU.mult), v)
        v = pv(lambda e: e.tensor_scalar(bh, bh, col(C_SH), None, ALU.mult), v)
        for b in range(B):
            v = pv(lambda e, b=b: e.tensor_copy(bhn.rearrange("p (c b) -> p c b", b=B)[:, :, b], bh[:, 8:12]), v)
        h03 = h0f.rearrange("p (c b) -> p c b", b=B)
        v_bias = v
        v = pv(lambda e: e.tensor_scalar(hst[1][:, :, 0], h03, col(SH_), None, ALU.mult), v)
        v = pv(lambda e: e.scalar_tensor_tensor(out=hst[1][:, :, 1], in0=h03, scalar=col(SH_),
                                                in1=hst[1][:, :, 0],
                                                op0=ALU.mult, op1=ALU.subtract), v)
        v = pv(lambda e: e.tensor_scalar(h0f, h0f, col(SH_), None, ALU.mult), v)
        v = pv(lambda e: e.tensor_scalar(wr_h[:, 0], wr_raw, col(SR), None, ALU.mult), v)
        v_small = pv(lambda e: e.scalar_tensor_tensor(out=wr_h[:, 1], in0=wr_raw, scalar=col(SR), in1=wr_h[:, 0],
                                                      op0=ALU.mult, op1=ALU.subtract), v)

        def split_group(src, hi, lo, scale, dep, last):
            v = pa(lambda e: e.activation(hi, src, ACT.Copy, scale=scale), dep, last)
            return pv(lambda e: e.scalar_tensor_tensor(out=lo, in0=src, scalar=scale, in1=hi,
                                                       op0=ALU.mult, op1=ALU.subtract), v)

        def halves(base, n):
            a = view(base, n * 1024, F16).rearrange("p (k s m) -> p k s m", s=2, m=512)
            return a[:, :, 0, :], a[:, :, 1, :]

        def group(base, shift, first, n, scale, dep, last):
            src = view(base + (shift + first) * CH, n * 512, F32).rearrange("p (k m) -> p k m", m=512)
            hi, lo = halves(base + first * CH, n)
            return split_group(src, hi, lo, scale, dep, last)

        v = v_sc
        for k in range(0, 12, 3):
            v = group(W_IH_OFF, 3, k, 3, col(SIH), v_ih, v)
        v_ihs = v
        v_xs = []
        for k in range(0, 16, 4):
            v = group(XR * CH, 4, k, 4, col(SX), v_x, v)
            v_xs.append(v)
        for k in range(0, 12, 3):
            v = group(W_HH * CH, 3, k, 3, col(SHH), v_hh, v)
        v_hhs = v
        v_pre = v
        v = rowmax(gcol[:, PGU:PGU + 1], raw(W_GU + 3, 24), v_gu)
        v = rowmax(gcol[:, PD:PD + 1], raw(W_GU + 27, 24), v_gu)
        v = pv(lambda e: e.tensor_tensor(gcol[:, PGU:PGU + 1], gcol[:, PGU:PGU + 1], gcol[:, PD:PD + 1], ALU.max), v)
        v = spread(PGU, 1, v)
        v = floors(PGU, 1, v)
        v = prod(C_TG, PGU, PH, 2.0 ** -29, v)
        for k in range(0, 48, 3):
            v = group(W_GU * CH, 3, k, 3, col(SGU), v_gu, v)
        v_gus = v

        PROD = ((0, 0), (0, 1), (1, 0))
        ihp = [psU[0], psU[1], psD[0], psD[1], psD[2], psD[3]]
        ev = [view(EV * CH + 2048 * k, 512, F32) for k in range(4)]
        v_ev, v_st = {}, {}
        n = 0
        for q in range(4):
            for fc in range(12):
                ps = ihp[n % 6]
                last = None
                for c in range(KC):
                    for i, (px, pw) in enumerate(PROD):
                        ih = view(W_IH_OFF + (c * 3 + fc // 4) * CH + pw * 1024, 512, F16)
                        w_ap = ih[:, (fc % 4) * 128:(fc % 4) * 128 + 128]
                        x_ap = half(XR + 4 * q + c, px)
                        st, sp_ = (c == 0 and i == 0), (c == KC - 1 and i == 2)
                        last = f.op("pe", lambda e, ps=ps, w_ap=w_ap, x_ap=x_ap, st=st, sp_=sp_:
                                    e.matmul(ps[:, :], w_ap, x_ap, start=st, stop=sp_),
                                    (v_ihs, v_xs[q], v_ev.get(n - 6)) if st else (), "gi_p" if sp_ else None)
                v_ev[n] = f.op("act", lambda e, n=n, ps=ps, fc=fc:
                               e.activation(ev[n % 4], ps[:, :], ACT.Identity, bias=bs[:, fc:fc + 1], scale=col(C_GI)),
                               (last, v_bias, v_st.get(n - 4)), "gi_a")
                v_st[n] = ld(gi_d[q, :, fc, :], ev[n % 4], f"st_gi{n % 4}", (v_ev[n],))
                n += 1
        v_gi_pe = last
        v_gi_act = v_ev[n - 1]
        v_gi_done = [v_st[n - 1 - k] for k in range(4)]

        for q in range(2):
            v_d = ld(raw(W_D + 3 + 12 * q, 12), wd[:, 6144 * q:6144 * (q + 1)], "ld_d", (v_gi_pe, *v_gi_done, v_gus))

        v_gil = {}

        def load_gi(s, free):
            off = (s * SUB * B) % 512
            v_gil[s] = ld(gi[s % 2], gi_d[(s * SUB * B) // 512, :, :, off:off + SUB * B], f"ld_gi{s % 2}",
                          (v_gi_pe, *v_gi_done, free))

        load_gi(0, None)
        load_gi(1, None)
        v_xyl = {}
        v_xys = {}

        def load_xy(b):
            q, o = b // 2, (b % 2) * 256
            src = x[:, 2048 * q:2048 * (q + 1)].rearrange("p (c n) -> p c n", c=KC)[:, :, o:o + 256]
            v_xyl[b] = ld(xy, src, "ld_xy", (v_gi_pe, v_xys.get(b - 1)))

        load_xy(0)

        gp = lambda fn, *w: f.op("pe", fn, w, "gru_p")
        gv = lambda fn, *w: f.op("dve", fn, w, "gru_v")
        ga = lambda fn, *w: f.op("act", fn, w, "gru_a")
        v_start = f.op("dve", lambda e: e.tensor_copy(Hs, h0f), (v_small, v_gi_pe), "gru_v")
        state = {"lo": v_start, "H": v_start}
        whv = []
        for c in range(KC):
            per = []
            for part in range(2):
                per.append(view(W_HH * CH + c * 3 * CH, 3 * 1024, F16)
                           .rearrange("p (g s c k) -> p g s c k", g=3, s=2, c=KC)[:, :, part])
            whv.append(per)
        v_hb_free = {}

        def step(t):
            b, tl = t // TB, t % TB
            prev = hst[(t + 1) % 2]
            first = True
            for c in range(KC):
                for part in range(2):
                    for j in range(4):
                        w_ap = whv[c][part][:, :, :, 32 * j:32 * j + 32]
                        l_ap = prev[:, c].rearrange("p s n -> p (s n)")
                        o_ap = psG[32 * j:32 * j + 16, 0:384]
                        fin = c == KC - 1 and part == 1 and j == 3
                        r = f.op("pe", lambda e, o_ap=o_ap, l_ap=l_ap, w_ap=w_ap, c=c, part=part, j=j:
                                 e.matmul(o_ap, l_ap, w_ap, start=(c == 0 and part == 0), stop=(c == KC - 1 and part == 1),
                                          tile_position=(0, 32 * j)),
                                 (state["lo"], v_hhs, v_psg) if first else (), "gru_p" if fin else None)
                        first = False
            v_mm = r
            s = t // SUB
            gt = gi[s % 2][:, :, (t % SUB) * B:(t % SUB) * B + B]
            Tf = Tt.rearrange("p f m -> p (f m)")
            v1 = gv(lambda e: e.transpose(Tf[:, 0:256], psG[:, 0:256]), v_mm)
            v2 = gv(lambda e: e.transpose(Tf[:, 256:384], psG[:, 256:384]))
            U3 = Uv.rearrange("p (f b) -> p f b", b=B)
            N3 = Un.rearrange("p (f b) -> p f b", b=B)
            v3 = gv(lambda e: e.tensor_tensor(U3, Tt[:, 0:8, 0:B], Tt[:, 0:8, B:2 * B], ALU.add), v1)
            v4 = gv(lambda e: e.tensor_tensor(U3, U3, gt[:, 0:8, :], ALU.add), v3, v_gil[s])
            a1 = ga(lambda e: e.activation(Uv, Uv, ACT.Tanh, scale=col(C_TR)), v4)
            v5 = gv(lambda e: e.tensor_tensor(N3, Tt[:, 8:12, 0:B], Tt[:, 8:12, B:2 * B], ALU.add), v2)
            v6 = gv(lambda e: e.tensor_tensor(Un, Un, bhn, ALU.add), v5)
            v7 = gv(lambda e: e.scalar_tensor_tensor(out=qq, in0=Uv[:, 0:32], scalar=1.0, in1=Un,
                                                     op0=ALU.add, op1=ALU.mult), a1, v6)
            v8 = gv(lambda e: e.scalar_tensor_tensor(out=ww.rearrange("p (c b) -> p c b", b=B),
                                                     in0=qq.rearrange("p (c b) -> p c b", b=B), scalar=0.5,
                                                     in1=gt[:, 8:12, :], op0=ALU.mult, op1=ALU.add), v7)
            a2 = ga(lambda e: e.activation(nn, ww, ACT.Tanh, scale=col(C_TN)), v8)
            v9 = gv(lambda e: e.tensor_scalar(zc, Uv[:, 32:64], col(C_MC1), col(C_C1), ALU.mult, ALU.add))
            v10 = gv(lambda e: e.scalar_tensor_tensor(out=zh, in0=Uv[:, 32:64], scalar=1.0, in1=Hs,
                                                      op0=ALU.add, op1=ALU.mult), state["H"])
            v11 = gv(lambda e: e.tensor_tensor(mm, zc, nn, ALU.mult), a2, v10)
            dst = hb[b % 2]
            hi, lo = hst[t % 2][:, :, 0], hst[t % 2][:, :, 1]
            c3 = lambda a: a.rearrange("p (c b) -> p c b", b=B)
            v12 = gv(lambda e: e.scalar_tensor_tensor(out=hi, in0=c3(zh), scalar=0.5, in1=c3(mm),
                                                      op0=ALU.mult, op1=ALU.add), v11)
            v13 = gv(lambda e: e.scalar_tensor_tensor(out=Hs, in0=zh, scalar=0.5, in1=mm,
                                                      op0=ALU.mult, op1=ALU.add))
            v14 = gv(lambda e: e.tensor_tensor(lo, c3(Hs), hi, ALU.subtract), v13)
            state["H"], state["lo"] = v13, v14
            state["kept"] = ga(lambda e: e.activation(dst[:, :, :, tl * B:tl * B + B].rearrange("p s c n -> p c s n"),
                                                      hst[t % 2], ACT.Copy), v14, v_hb_free.get(b - 2))
            if (t + 1) % SUB == 0 and s + 2 < T // SUB:
                load_gi(s + 2, v8)

        work = []
        v_u_free = [None, None]
        v_x_free = [None, None]
        v_ah_free = [None, None]
        v_cb_free = [v_gi_act]
        v_d_free = [v_gi_act] * 4
        turn = [0]
        d_state = {"done": None}

        def fv(fn, *w):
            return f.op("dve", fn, w, "ffn_v")

        def fa(fn, *w):
            return f.op("act", fn, w, "ffn_a")

        def ffn(b, v_h):
            hh = hb[b % 2]

            def mm_(out, l_ap, r_ap, st, sp_, waits, post):
                return f.op("pe", lambda e: e.matmul(out, l_ap, r_ap, start=st, stop=sp_), waits,
                            "ffn_p" if post else None)

            for tc in range(2):
                for c in range(KC):
                    for i, (ph, pw) in enumerate(PROD):
                        st, sp_ = (c == 0 and i == 0), (c == KC - 1 and i == 2)
                        v_lg = mm_(psM[:, tc * 8:tc * 8 + 8], hh[:, ph, c, tc * 128:tc * 128 + 128],
                                   wr_h[:, pw, c * 8:c * 8 + 8], st, sp_,
                                   (v_h, v_cb_free[0], v_small) if st else (), sp_)
                        yield 60.0
            route = {}

            def router():
                lg = psM[:, 0:16]
                m8, pr, p8, t1, t2 = (rt[:, 16 * k:16 * k + 16] for k in range(5))
                fi = rt[:, 80:96]
                w2 = rt[:, 96:112]
                sm = rt[:, 112:128]

                def one(tc):
                    o = slice(8 * tc, 8 * tc + 8)
                    k = 2 * tc
                    v = fv(lambda e: e.max(m8[:, o], lg[:, o]), v_lg)
                    v = fv(lambda e: e.tensor_scalar(sm[:, k:k + 1], m8[:, 8 * tc:8 * tc + 1], col(C_MIR), None, ALU.mult), v)
                    a = fa(lambda e: e.activation(pr[:, o], lg[:, o], ACT.Exp, bias=sm[:, k:k + 1], scale=col(C_IR),
                                                  accum_out=sm[:, k + 1:k + 2]), v)
                    v = fv(lambda e: e.reciprocal(sm[:, 8 + k:9 + k], sm[:, k + 1:k + 2]), a)
                    v = fv(lambda e: e.tensor_scalar(pr[:, o], pr[:, o], sm[:, 8 + k:9 + k], None, ALU.mult), v)
                    v = fv(lambda e: e.max(p8[:, o], pr[:, o]), v)
                    vi = fv(lambda e: e.max_index(idx[:, o], p8[:, o], pr[:, o]), v)
                    vi = fv(lambda e: e.tensor_copy(fi[:, o], idx[:, o]), vi)
                    v = fv(lambda e: e.tensor_tensor(sm[:, 9 + k:10 + k], p8[:, 8 * tc:8 * tc + 1],
                                                     p8[:, 8 * tc + 1:8 * tc + 2], ALU.add), vi)
                    v = fv(lambda e: e.reciprocal(sm[:, 9 + k:10 + k], sm[:, 9 + k:10 + k]), v)
                    v = fv(lambda e: e.tensor_scalar(pr[:, o], pr[:, o], sm[:, 9 + k:10 + k], CB, ALU.mult, ALU.mult), v)
                    v = fv(lambda e: e.tensor_scalar(t1[:, o], iot, fi[:, 8 * tc:8 * tc + 1], None, ALU.is_equal), v)
                    v = fv(lambda e: e.scalar_tensor_tensor(out=t2[:, o], in0=iot, scalar=fi[:, 8 * tc + 1:8 * tc + 2],
                                                            in1=t1[:, o], op0=ALU.is_equal, op1=ALU.add), v)
                    v = fv(lambda e: e.tensor_tensor(w2[:, o], pr[:, o], t2[:, o], ALU.mult), v)
                    v = fv(lambda e: e.tensor_copy(cmb[:, tc, 0], w2[:, o]), v, v_cmb_free[0])
                    v = fv(lambda e: e.tensor_tensor(cmb[:, tc, 1], w2[:, o], cmb[:, tc, 0], ALU.subtract), v)
                    return v

                one(0)
                route["v"] = one(1)

            work.append((3000, router))
            order = list(range(16, 24)) + list(range(16))
            done = {}

            def unit_cb(i):
                e_ = i // 2
                for tc in range(2):
                    for s in range(2):
                        l_ap = cmb[:, tc, s, e_:e_ + 1].broadcast_to([P, 128])
                        last = tc == 1 and s == 1
                        r = mm_(psM[:, 128 * tc:128 * tc + 128], l_ap, idh, s == 0, s == 1,
                                (route["v"], v_cb_free[0]), last)
                        if last:
                            route[e_] = r
                            v_cmb_free[0] = r
                        yield 60.0

            def unit_gu(n_, i, ready):
                k = turn[0] % 2
                turn[0] += 1
                if i < 16:
                    cols = ((i // 2, (i % 2) * 128), (i // 2, 256 + (i % 2) * 128))
                else:
                    s = i - 16
                    cols = ((8 + s // 4, (s % 4) * 128), (10 + s // 4, (s % 4) * 128))
                for gu, (e_, o) in enumerate(cols):
                    for c in range(KC):
                        for j, (ph, pw) in enumerate(PROD):
                            st, sp_ = (c == 0 and j == 0), (c == KC - 1 and j == 2)
                            w_ap = half(W_GU + c * 12 + e_, pw)[:, o:o + 128]
                            r = mm_(psU[k][:, 256 * gu:256 * gu + 256], w_ap, hh[:, ph, c, :], st, sp_,
                                    (v_h, v_u_free[k], v_gus, v_gi_act) if st else (), sp_ and gu == 1)
                            yield 109.0

                def elementwise():
                    t_ = X[k]
                    g, u = psU[k][:, 0:256], psU[k][:, 256:512]
                    a = fa(lambda e: e.activation(t_, g, ACT.Tanh, scale=col(C_TG)), r, v_x_free[k])
                    v = fv(lambda e: e.scalar_tensor_tensor(out=t_, in0=t_, scalar=1.0, in1=g,
                                                            op0=ALU.add, op1=ALU.mult), a)
                    al = A_RT if i < 16 else A_SH
                    v = fv(lambda e: e.scalar_tensor_tensor(out=t_, in0=t_, scalar=al, in1=u,
                                                            op0=ALU.mult, op1=ALU.mult), v)
                    v_u_free[k] = v
                    if i < 16:
                        v = fv(lambda e: e.tensor_tensor(t_, t_, psM[:, 0:256], ALU.mult), v, route[i // 2])
                        v_cb_free[0] = v
                    v = fv(lambda e: e.tensor_copy(AH[k][:, 0], t_), v, v_ah_free[k])
                    v = fv(lambda e: e.tensor_tensor(AH[k][:, 1], t_, AH[k][:, 0], ALU.subtract), v)
                    v_x_free[k] = v
                    done[n_] = (v, k)

                ready.append(elementwise)

            def unit_down(n_, i):
                v, k = done[n_]
                for hc in range(4):
                    for j, (pa_, pw) in enumerate(PROD):
                        st, sp_ = (n_ == 0 and j == 0), (n_ == 23 and j == 2)
                        w_ap = half(W_D + i, pw)[:, hc * 128:hc * 128 + 128]
                        r = mm_(psD[hc][:, 0:256], w_ap, AH[k][:, pa_, :], st, sp_,
                                (v, v_ds[0], v_d_free[hc]) if j == 0 else (), hc == 3 and j == 2)
                        yield 109.0
                v_ah_free[k] = r
                if n_ == 23:
                    def finish():
                        for hc in range(4):
                            v = fv(lambda e, hc=hc: e.scalar_tensor_tensor(
                                out=xy[:, hc, :], in0=psD[hc][:, 0:256], scalar=col(C_OUT), in1=xy[:, hc, :],
                                op0=ALU.mult, op1=ALU.add), r, v_xyl[b])
                            v_d_free[hc] = v
                        v_xys[b] = ld(y[:, :, b * 256:(b + 1) * 256], xy, "st_y", (v,))
                        if b + 1 < NBLK:
                            load_xy(b + 1)
                        d_state["done"] = b

                    work.append((1400, finish))

            for n_, i in enumerate(order):
                ready = []
                yield from unit_gu(n_, i, ready)
                if i >= 16:
                    work.append((1700, ready[0]))
                if n_:
                    while n_ - 1 not in done:
                        yield None
                    yield from unit_down(n_ - 1, order[n_ - 1])
                if i < 16:
                    if i % 2 == 0:
                        while "v" not in route:
                            yield None
                        yield from unit_cb(i)
                    work.append((2100, ready[0]))
            while 23 not in done:
                yield None
            v_hb_free[b] = ("ffn_p", f.count["ffn_p"])
            yield from unit_down(23, order[23])
            while d_state["done"] != b:
                yield None

        v_cmb_free = [None]

        v_ds = [None]

        def prep_down():
            acc = {}

            def m(k):
                acc[k] = rowmax(mx[:, k:k + 1], raw(W_D + 3 + k, 1), v_d)

            for k in range(24):
                work.append((620, lambda k=k: m(k)))

            def g():
                v = rowmax(gcol[:, PD:PD + 1], mx[:, 0:24], acc[23])
                v = spread(PD, 1, v)
                v = floors(PD, 1, v)
                v = prod(C_T0, PGU, PH, 2.0 ** 3, v)
                v = prod(C_T1, C_T0, C_T0, 1.0, v)
                acc["g"] = prod(C_OUT, PD, C_T1, 2.0 ** -13, v)

            work.append((2500, g))

            def s(k):
                acc["g"] = group(W_D * CH, 3, k, 1, col(SD), v_d, acc["g"])
                if k == 23:
                    v_ds[0] = acc["g"]

            for k in range(24):
                work.append((700, lambda k=k: s(k)))

        prep_down()

        def do_work(budget):
            while work and budget > 0:
                c, fn = work.pop(0)
                fn()
                budget -= c

        blocks = []
        current = [None]

        def fill(budget):
            while budget > 0:
                if current[0] is None:
                    if not blocks:
                        return
                    current[0] = blocks.pop(0)
                c = next(current[0], "end")
                if c == "end":
                    current[0] = None
                    continue
                if c is None:
                    return
                budget -= c

        for t in range(T):
            step(t)
            fill(QUOTA)
            do_work(2000.0)
            if (t + 1) % TB == 0:
                blocks.append(ffn(t // TB, state["kept"]))
                if t < TB:
                    do_work(1e9)
        while blocks or current[0] is not None or work:
            fill(2700.0)
            do_work(2500.0)

        block = ctx.enter_context(nc.Block())

        @block.sync
        def _(e):
            f.play("sp", e)
            for s in ("st_gi0", "st_gi1", "st_gi2", "st_gi3", "st_y"):
                e.wait_ge(f.sems[s], f.count[s])

        @block.tensor
        def _(e):
            f.play("pe", e)

        @block.vector
        def _(e):
            f.play("dve", e)

        @block.scalar
        def _(e):
            f.play("act", e)


def kernel(x, cond_2048, L0_cond_W_ih, L0_cond_W_hh, L0_cond_b_ih, L0_cond_b_hh, L0_ffn_w_gate,
           L0_ffn_w_gate_up, L0_ffn_w_down, L0_ffn_w_sh_gate_up, L0_ffn_w_sh_down):
    import concourse.bacc as _bacc
    from concourse.bass_utils import run_bass_kernel_spmd as _run

    c = np.ascontiguousarray

    def rows(w):
        k, m = w.shape
        return np.asarray(w).reshape(k // 128, 128, m).transpose(1, 0, 2)

    arrays = {
        "x": c(np.asarray(x).transpose(2, 1, 0).reshape(4, 128, 4, 512).transpose(1, 2, 0, 3).reshape(128, 8192)),
        "h0": c(rows(np.asarray(cond_2048).T).reshape(128, 32)),
        "wih": c(rows(L0_cond_W_ih).reshape(128, 6144)),
        "whh": c(rows(L0_cond_W_hh).reshape(128, 6144)),
        "bih": c(np.asarray(L0_cond_b_ih).reshape(12, 128).T),
        "bhh": c(np.asarray(L0_cond_b_hh).reshape(12, 128).T),
        "wr": c(rows(L0_ffn_w_gate).reshape(128, 32)),
        "wgu": c(np.concatenate([np.asarray(L0_ffn_w_gate_up).reshape(8, 4, 128, 512).transpose(2, 1, 0, 3),
                                 rows(L0_ffn_w_sh_gate_up).reshape(128, 4, 4, 512)], axis=2).reshape(128, 24576)),
        "wd": c(np.concatenate([rows(np.asarray(L0_ffn_w_down).reshape(2048, 512)), rows(L0_ffn_w_sh_down)],
                               axis=1).reshape(128, 12288)),
        "ident": np.eye(128, dtype=np.float32),
        "iota": c(np.broadcast_to(np.arange(8, dtype=np.float32), (128, 8))),
    }
    nc = _bacc.Bacc("TRN2", target_bir_lowering=False, num_devices=1)
    args = [nc.dram_tensor(n, a.shape, mybir.dt.from_np(a.dtype), kind="ExternalInput").ap()
            for n, a in arrays.items()]
    out = nc.dram_tensor("y", (128, 4, 2048), F32, kind="ExternalOutput").ap()
    adaln_ffn(nc, *args, out)
    r = _run(nc, [arrays], core_ids=[0])
    got = r.results[0]["y"]
    return c(got.transpose(1, 0, 2).reshape(512, 256, 8).transpose(2, 1, 0))
```

```python
from contextlib import ExitStack

import numpy as np

import concourse.bass as bass
from concourse import mybir

ALU = mybir.AluOpType
ACT = mybir.ActivationFunctionType
AX = mybir.AxisListType
F32 = mybir.dt.float32
F16 = mybir.dt.float16
U32 = mybir.dt.uint32
U8 = mybir.dt.uint8

P = 128
B, T, D = 8, 256, 512
KC = 4
E = 8
TB = 32
NBLK = T // TB
N = TB * B
SUB = 16
CH = 2048
NCHUNK = 24
A_SH = 2.0 ** -64
A_RT = 2.0 ** -74
CB = 1024.0
QUOTA = 3000.0
WINDOW = 2000.0
PRE_MAX = 12
QUOTA_F = 3050.0
CATCH_UP = 3600.0


class Flow:

    def __init__(self, nc, ctx):
        self.nc, self.ctx = nc, ctx
        self.q = {k: [] for k in ("pe", "dve", "act", "sp")}
        self.count = {}
        self.sems = {}

    def sem(self, name):
        self.sems[name] = self.ctx.enter_context(self.nc.semaphore(name))
        self.count[name] = 0
        return name

    def op(self, eng, fn, waits=(), post=None, by=1):
        if post is not None:
            self.count[post] += by
        self.q[eng].append((tuple(w for w in waits if w is not None), fn, post, by))
        return (post, self.count[post]) if post is not None else None

    def play(self, eng, e):
        met = {}
        for waits, fn, post, by in self.q[eng]:
            need = {}
            for s, v in waits:
                need[s] = max(need.get(s, 0), v)
            for s, v in need.items():
                if met.get(s, 0) < v:
                    e.wait_ge(self.sems[s], v)
                    met[s] = v
            ins = fn(e)
            if post is not None:
                ins.then_inc(self.sems[post], by)


def adaln_ffn(nc, x, h0, wih, whh, bih, bhh, wr, wgu, wd, ident, iota, y):
    with ExitStack() as ctx:
        f = Flow(nc, ctx)

        def psum(name):
            return ctx.enter_context(nc.psum_tensor(name, [P, 512], F32))

        arena = ctx.enter_context(nc.sbuf_tensor("arena", [P, 212800], U8))
        gi_d = nc.dram_tensor("gi_scratch", [NBLK, P, 12, N], F32)

        def view(off, n, dt):
            size = 2 if dt == F16 else 4
            return arena[:, off:off + n * size].bitcast(dt)

        psG = psum("psG")
        psM = psum("psM")
        psU = [psum("psU0"), psum("psU1")]
        psD = [psum(f"psD{i}") for i in range(4)]

        SHIFT = 2
        W_HH, W_GU, W_D = 0, 12, 60
        W_IH = 60 + SHIFT
        XP = [W_IH + 12 + SHIFT + 3 * k for k in range(2)]
        EV = XP[1] + 3
        XALL = W_GU + SHIFT + 32
        U0 = 87 * CH

        def raw(slot, n):
            return view(slot * CH, n * 512, F32)

        def half(slot, part):
            return view(slot * CH + part * 1024, 512, F16)

        hb = [view(U0 + 4096 * k, 2048, F16).rearrange("p (s c n) -> p s c n", s=2, c=KC) for k in range(2)]
        gi = [view(U0 + 8192 + 6144 * k, 1536, F32).rearrange("p (f n) -> p f n", f=12) for k in range(2)]
        xy = view(U0 + 20480, 1024, F32).rearrange("p (c n) -> p c n", c=KC)
        X = [view(o, 256, F32) for o in (U0 + 24576, U0 + 25600, 86 * CH)]
        AH = [view(o, 512, F16).rearrange("p (s n) -> p s n", s=2) for o in (U0 + 26624, U0 + 27648, 86 * CH + 1024)]
        g0 = U0 + 28672
        Tt = view(g0, 384, F32).rearrange("p (f m) -> p f m", f=12)
        g0 += 1536
        Hs, zh, mm, qq, ww, nn, zc, nc1 = [view(g0 + 128 * k, 32, F32) for k in range(8)]
        g0 += 1024
        c0 = U0 + 31232
        idf = view(c0, 128, F32)
        idh = view(c0 + 512, 128, F16)
        sc = view(c0 + 768, 32, F32)
        iot = view(c0 + 896, 8, F32)
        bi = view(c0 + 928, 12, F32)
        bh = view(c0 + 976, 12, F32)
        bs = view(c0 + 1024, 12, F32)
        bhn = view(c0 + 1072, 32, F32)
        wr_raw = view(c0 + 1200, 32, F32)
        wr_h = view(c0 + 1328, 64, F16).rearrange("p (s n) -> p s n", s=2)
        h0f = view(c0 + 1456, 32, F32)
        hst = [view(c0 + 1584 + 128 * k, 64, F16).rearrange("p (c s n) -> p c s n", s=2, c=KC) for k in range(2)]
        mx = view(c0 + 1840, 64, F32)
        gcol = view(c0 + 2096, 16, F32)
        rt = view(c0 + 2160, 128, F32)
        cmb = view(c0 + 2672, 32, F16).rearrange("p (t s e) -> p t s e", t=2, s=2)
        idx = view(c0 + 2736, 16, U32)
        Uv = view(c0 + 2800, 96, F32)
        assert c0 + 3184 <= 212800 and g0 <= c0

        for n_ in ("ld_a", "ld_x", "ld_ih", "ld_hh", "ld_gu0", "ld_gu1", "ld_gu2", "ld_gu3", "ld_d", "ld_gi0",
                   "ld_gi1", "ld_xy", "ld_xp0", "ld_xp1", "st_y", "prep_v", "prep_a", "prep_p", "gi_p", "gi_a",
                   "gru_p", "gru_v", "gru_a", "ffn_p", "ffn_v", "ffn_a"):
            f.sem(n_)
        for k in range(8):
            f.sem(f"st_gi{k}")

        def ld(out, in_, post, *waits):
            return f.op("sp", lambda e: e.dma_start(out, in_), waits, post, 16)

        def pv(fn, *waits):
            return f.op("dve", fn, waits, "prep_v")

        def pa(fn, *waits):
            return f.op("act", fn, waits, "prep_a")

        def col(k):
            return sc[:, k:k + 1]

        (PX, PIH, PHH, PR, PH, PGU, PD) = range(7)
        SX, SIH, SHH, SR, SH_, SGU, SD = range(8, 15)
        (C_SH, C_TR, C_TN, C_GI, C_NC1, C_IR, C_MIR, C_TG, C_OUT, C_T0, C_T1) = range(16, 27)

        v_ih = [ld(raw(W_IH + SHIFT + 6 * q, 6), wih[:, 3072 * q:3072 * (q + 1)], "ld_ih") for q in range(2)][-1]
        v_x = ld(raw(XALL, 16), x, "ld_x")
        v_hh = ld(raw(W_HH + SHIFT, 12), whh, "ld_hh")
        for out, src in ((idf, ident), (iot, iota), (bi, bih), (bh, bhh), (wr_raw, wr), (h0f, h0)):
            v_a = ld(out, src, "ld_a")
        v_xp, v_xs, v_gi_piece, v_st = {}, {}, {}, {}

        def load_xp(p):
            v_xp[p] = ld(raw(XP[p % 2] + 1, 2), x[:, 1024 * p:1024 * (p + 1)], f"ld_xp{p % 2}", v_gi_piece.get(p - 2))

        load_xp(0)
        load_xp(1)
        v_gu = [ld(raw(W_GU + SHIFT + 12 * q, 12), wgu[:, 6144 * q:6144 * (q + 1)], f"ld_gu{q}") for q in range(2)]

        def rowmax(out, in_, *waits):
            return pv(lambda e: e.tensor_reduce(out, in_, AX.X, ALU.max, apply_absolute_value=True), *waits)

        def rowsum(out, in_, *waits):
            return pa(lambda e: e.activation(in_, in_, ACT.Abs, accum_out=out), *waits)

        def spread(k0, nk, *dep):
            v = f.op("pe", lambda e: e.matmul(psM[0:nk, 0:128], gcol[:, k0:k0 + nk], idf[:, :], start=True, stop=True),
                     (*dep, v_a), "prep_p")
            v = pv(lambda e: e.tensor_reduce(mx[0:nk, 40:41], psM[0:nk, 0:128], AX.X, ALU.max), v)
            v = f.op("pe", lambda e: e.matmul(psM[:, 0:nk], mx[0:nk, 40:41].broadcast_to([nk, 128]), idf[0:nk, 0:nk],
                                              start=True, stop=True), (v,), "prep_p")
            return pv(lambda e: e.tensor_scalar(sc[:, k0:k0 + nk], psM[:, 0:nk], 2.0 ** -40, None, ALU.max), v)

        def floors(k0, nk, v):
            bits = sc[:, k0:k0 + nk].bitcast(U32)
            v = pv(lambda e: e.tensor_scalar(bits, bits, 0x7F800000, None, ALU.bitwise_and), v)
            v = pv(lambda e: e.reciprocal(sc[:, 8 + k0:8 + k0 + nk], sc[:, k0:k0 + nk]), v)
            return pv(lambda e: e.tensor_scalar(sc[:, 8 + k0:8 + k0 + nk], sc[:, 8 + k0:8 + k0 + nk],
                                                2.0 ** 14, None, ALU.mult), v)

        def prod(out, a, b, k, v):
            return pv(lambda e: e.scalar_tensor_tensor(out=col(out), in0=col(a), scalar=k, in1=col(b),
                                                       op0=ALU.mult, op1=ALU.mult), v)

        for k in range(4):
            v_xsum = rowsum(mx[:, k:k + 1], raw(XALL + 4 * k, 4), v_x)
        v_gu += [ld(raw(W_GU + SHIFT + 12 * q, 12), wgu[:, 6144 * q:6144 * (q + 1)], f"ld_gu{q}", v_xsum)
                 for q in range(2, 4)]
        v_psg = pv(lambda e: e.memset(psG[:, :], 0.0))
        rowmax(gcol[:, PIH:PIH + 1], raw(W_IH + SHIFT, 12), v_ih)
        rowmax(gcol[:, PHH:PHH + 1], raw(W_HH + SHIFT, 12), v_hh)
        rowmax(gcol[:, PR:PR + 1], wr_raw, v_a)
        rowmax(gcol[:, PH:PH + 1], h0f, v_a)
        v = rowmax(gcol[:, PX:PX + 1], mx[:, 0:4], v_xsum)
        v = spread(0, 5, v)
        v = pv(lambda e: e.tensor_scalar(col(PH), col(PH), 1.0, None, ALU.max), v)
        v_sc = v = floors(0, 5, v)

        def split(dst, shift, scale, dep, *free):
            src = raw(dst + shift, 1)
            hi, lo = half(dst, 0), half(dst, 1)
            v = pa(lambda e: e.activation(hi, src, ACT.Copy, scale=scale), dep, *free)
            return pv(lambda e: e.scalar_tensor_tensor(out=lo, in0=src, scalar=scale, in1=hi,
                                                       op0=ALU.mult, op1=ALU.subtract), v)

        def split_row(base, n, scale, dep, v):
            old = [v] * SHIFT
            for k in range(n):
                old.append(split(base + k, SHIFT, scale, dep, old[-SHIFT]))
            return old[-1]

        def split_xp(p):
            v = v_sc
            for k in range(2):
                v = split(XP[p % 2] + k, 1, col(SX), v_xp[p], v, v_gi_piece.get(p - 2))
            v_xs[p] = v

        split_xp(0)
        v_ihs = split_row(W_IH, 12, col(SIH), v_ih, v_sc)
        v = prod(C_SH, SHH, SH_, 1.0, v_sc)
        v = prod(C_TN, PHH, PH, 2.0 ** -28, v)
        v = pv(lambda e: e.tensor_scalar(col(C_TR), col(C_TN), 0.5, None, ALU.mult), v)
        v = prod(C_T0, PX, PIH, 2.0 ** -28, v)
        v = prod(C_GI, C_T0, C_SH, 1.0, v)
        v = prod(C_IR, PR, PH, 2.0 ** -28, v)
        v = prod(C_MIR, PR, PH, -(2.0 ** -28), v)
        v = pv(lambda e: e.tensor_tensor(bs[:, 0:12], bi[:, 0:12], bh[:, 0:12], ALU.add), v)
        v = pv(lambda e: e.tensor_copy(bs[:, 4:8], bi[:, 4:8]), v)
        v = pv(lambda e: e.tensor_scalar(bs, bs, col(C_SH), None, ALU.mult), v)
        v_bias = v
        split_xp(1)
        v_hhs = split_row(W_HH, 12, col(SHH), v_hh, v_sc)
        v = pv(lambda e: e.tensor_scalar(bh, bh, col(C_SH), None, ALU.mult), v_bias)
        c3 = lambda a: a.rearrange("p (c b) -> p c b", b=B)
        for b in range(B):
            v = pv(lambda e, b=b: e.tensor_copy(c3(bhn)[:, :, b], bh[:, 4:8]), v)
        v = pv(lambda e: e.tensor_copy(idh, idf), v_a)
        h03 = c3(h0f)
        v = pv(lambda e: e.tensor_scalar(hst[1][:, :, 0], h03, col(SH_), None, ALU.mult), v)
        v = pv(lambda e: e.scalar_tensor_tensor(out=hst[1][:, :, 1], in0=h03, scalar=col(SH_), in1=hst[1][:, :, 0],
                                                op0=ALU.mult, op1=ALU.subtract), v)
        v = pv(lambda e: e.tensor_scalar(Hs, h0f, col(SH_), None, ALU.mult), v)
        v = pv(lambda e: e.memset(nc1, -0.5), v)
        v = pv(lambda e: e.tensor_scalar(nc1, nc1, col(SH_), None, ALU.mult), v)
        v = pv(lambda e: e.tensor_scalar(wr_h[:, 0], wr_raw, col(SR), None, ALU.mult), v)
        v_small = pv(lambda e: e.scalar_tensor_tensor(out=wr_h[:, 1], in0=wr_raw, scalar=col(SR), in1=wr_h[:, 0],
                                                      op0=ALU.mult, op1=ALU.subtract), v)

        PROD = ((0, 0), (0, 1), (1, 0))

        act_now = []
        late_dve = []
        ew = []
        work = []

        gi_ps = [psU[0], psU[1], *psD]
        ev = [view(EV * CH + 1024 * k, 256, F32) for k in range(8)]
        v_ev, v_evs = {}, {}

        def input_gates(p):
            while p not in v_xs:
                yield None
            for fc in range(12):
                n = 12 * p + fc
                ps = gi_ps[n % 6][:, 0:N]
                while n >= 6 and n - 6 not in v_ev:
                    yield None
                for c in range(KC):
                    for i, (px, pw) in enumerate(PROD):
                        w_ap = half(W_IH + c * 3 + fc // 4, pw)[:, (fc % 4) * 128:(fc % 4) * 128 + 128]
                        x_ap = half(XP[p % 2] + c // 2, px)[:, (c % 2) * 256:(c % 2) * 256 + 256]
                        st, sp_ = (c == 0 and i == 0), (c == KC - 1 and i == 2)
                        r = f.op("pe", lambda e, ps=ps, w_ap=w_ap, x_ap=x_ap, st=st, sp_=sp_:
                                 e.matmul(ps, w_ap, x_ap, start=st, stop=sp_),
                                 (v_ihs, v_xs[p], v_ev.get(n - 6)) if st else (), "gi_p" if sp_ else None)
                        yield 109.0

                def evacuate(n=n, fc=fc, ps=ps, r=r):
                    v_ev[n] = f.op("act", lambda e: e.activation(ev[n % 8], ps, ACT.Identity, bias=bs[:, fc:fc + 1],
                                                                 scale=col(C_GI)),
                                   (r, v_bias, v_evs.get(n - 8)), "gi_a")
                    v_evs[n] = ld(gi_d[p, :, fc, :], ev[n % 8], f"st_gi{n % 8}", v_ev[n])
                    v_st.setdefault(p, []).append(v_evs[n])

                act_now.append(evacuate)
            v_gi_piece[p] = r
            if p + 2 < NBLK:
                load_xp(p + 2)
                work.insert(0, (1500, lambda: split_xp(p + 2)))
            if p == NBLK - 1:
                while len(v_st.get(p, ())) < 12:
                    yield None
                stored = [w for q in v_st.values() for w in q]
                for q in range(4):
                    v_d.append(ld(raw(W_D + SHIFT + 6 * q, 6), wd[:, 3072 * q:3072 * (q + 1)], "ld_d", r, *v_gus, *stored))
                load_xy(0)

        v_d, v_gus, v_gs, v_ds = [], [], {}, {}
        v_gil, v_xyl, v_xys = {}, {}, {}

        def load_gi(s, free):
            off = (s * SUB * B) % N
            p = (s * SUB * B) // N
            assert len(v_st[p]) == 12
            v_gil[s] = ld(gi[s % 2], gi_d[p, :, :, off:off + SUB * B], f"ld_gi{s % 2}", *v_st[p], free)

        def load_xy(b):
            v_xyl[b] = ld(xy, x[:, 1024 * b:1024 * (b + 1)].rearrange("p (c n) -> p c n", c=KC), "ld_xy", v_xys.get(b - 1))

        def max_gu(k):
            v_mgu.append(rowmax(mx[:, k:k + 1], raw(W_GU + SHIFT + 2 * k, 2), v_gu[k // 6]))

        v_mgu = []

        def prep_gu():
            for k in range(PRE_MAX, 24):
                work.append((1150, lambda k=k: max_gu(k)))
            state_ = {}

            def scale():
                v = rowmax(gcol[:, PGU:PGU + 1], mx[:, 0:24], v_mgu[-1])
                v = spread(PGU, 1, v)
                v = floors(PGU, 1, v)
                state_["old"] = [prod(C_TG, PGU, PH, 2.0 ** -29, v)] * SHIFT

            work.append((2500, scale))

            def one(k):
                old = state_["old"]
                old.append(split(W_GU + k, SHIFT, col(SGU), v_gu[k // 12], old[-SHIFT]))
                if k % 4 == 3:
                    v_gs[k // 4] = old[-1]
                if k == 47:
                    v_gus.append(old[-1])

            for k in range(48):
                work.append((640, lambda k=k: one(k)))

        def prep_down():
            state_ = {}

            def bound(k):
                state_["b"] = pa(lambda e: e.activation(raw(W_D, 1), raw(W_D + SHIFT + k, 1), ACT.Abs,
                                                        accum_out=mx[:, k:k + 1]), v_d[-1], state_.get("b"))

            for k in range(24):
                work.append((600, lambda k=k: bound(k)))

            def scale():
                v = rowmax(gcol[:, PD:PD + 1], mx[:, 0:24], state_["b"])
                v = spread(PD, 1, v)
                v = floors(PD, 1, v)
                v = prod(C_T0, PGU, PH, 2.0 ** 3, v)
                v = prod(C_T1, C_T0, C_T0, 1.0, v)
                state_["old"] = [prod(C_OUT, PD, C_T1, 2.0 ** -13, v)] * SHIFT

            work.append((2500, scale))

            def one(k):
                old = state_["old"]
                old.append(split(W_D + k, SHIFT, col(SD), v_d[-1], old[-SHIFT]))
                v_ds[k] = old[-1]

            for k in range(24):
                work.append((640, lambda k=k: one(k)))

        gv = lambda fn, *w: f.op("dve", fn, w, "gru_v")
        ga = lambda fn, *w: f.op("act", fn, w, "gru_a")
        state = {"lo": v_small, "H": v_small, "zh": None}
        whv = [[view((W_HH + c * 3) * CH, 3 * 1024, F16)
                .rearrange("p (g s c k) -> p g s c k", g=3, s=2, c=KC)[:, :, part] for part in range(2)]
               for c in range(KC)]
        v_hb_free = {}
        Tf = Tt.rearrange("p f m -> p (f m)")
        U3 = c3(Uv)
        Ur, Un, Uz = Uv[:, 0:32], Uv[:, 32:64], Uv[:, 64:96]

        def step_pe(t):
            prev = hst[(t + 1) % 2]
            first = True
            for c in range(KC):
                for part in range(2):
                    for j in range(4):
                        w_ap = whv[c][part][:, :, :, 32 * j:32 * j + 32]
                        l_ap = prev[:, c].rearrange("p s n -> p (s n)")
                        o_ap = psG[32 * j:32 * j + 16, 0:384]
                        fin = c == KC - 1 and part == 1 and j == 3
                        r = f.op("pe", lambda e, o_ap=o_ap, l_ap=l_ap, w_ap=w_ap, c=c, part=part, j=j:
                                 e.matmul(o_ap, l_ap, w_ap, start=(c == 0 and part == 0), stop=(c == KC - 1 and part == 1),
                                          tile_position=(0, 32 * j)),
                                 (state["lo"], v_hhs, v_psg) if first else (), "gru_p" if fin else None)
                        first = False
            return r

        def step(t, v_mm):
            b, tl = t // TB, t % TB
            s = t // SUB
            gt = gi[s % 2][:, :, (t % SUB) * B:(t % SUB) * B + B]
            new = hst[t % 2]
            t_r = gv(lambda e: e.transpose(Tf[:, 0:128], psG[:, 0:128]), v_mm)
            t_nz = gv(lambda e: e.transpose(Tf[:, 128:384], psG[:, 128:384]))
            u_r = gv(lambda e: e.tensor_tensor(U3[:, 0:4], Tt[:, 0:4, 0:B], Tt[:, 0:4, B:2 * B], ALU.add), t_r)
            u_nz = gv(lambda e: e.tensor_tensor(U3[:, 4:12], Tt[:, 4:12, 0:B], Tt[:, 4:12, B:2 * B], ALU.add), t_nz)
            g_r = gv(lambda e: e.tensor_tensor(U3[:, 0:4], U3[:, 0:4], gt[:, 0:4, :], ALU.add), u_r, v_gil[s])
            s_r = ga(lambda e: e.activation(Ur, Ur, ACT.Tanh, scale=col(C_TR)), g_r)
            g_z = gv(lambda e: e.tensor_tensor(U3[:, 8:12], U3[:, 8:12], gt[:, 8:12, :], ALU.add), u_nz)
            s_z = ga(lambda e: e.activation(Uz, Uz, ACT.Tanh, scale=col(C_TR)), g_z)
            b_n = gv(lambda e: e.tensor_tensor(Un, Un, bhn, ALU.add), u_nz)
            q_ = gv(lambda e: e.scalar_tensor_tensor(out=qq, in0=Ur, scalar=1.0, in1=Un, op0=ALU.add, op1=ALU.mult),
                    s_r, b_n)
            zc_ = gv(lambda e: e.scalar_tensor_tensor(out=zc, in0=Uz, scalar=-1.0, in1=nc1, op0=ALU.add, op1=ALU.mult),
                     s_z)
            w_ = gv(lambda e: e.scalar_tensor_tensor(out=c3(ww), in0=c3(qq), scalar=0.5, in1=gt[:, 4:8, :],
                                                     op0=ALU.mult, op1=ALU.add), q_)
            s_n = ga(lambda e: e.activation(nn, ww, ACT.Tanh, scale=col(C_TN)), w_)
            zh_ = gv(lambda e: e.scalar_tensor_tensor(out=zh, in0=Uz, scalar=1.0, in1=Hs, op0=ALU.add, op1=ALU.mult),
                     state["H"])
            m_ = gv(lambda e: e.tensor_tensor(mm, zc, nn, ALU.mult), s_n, zc_)
            while act_now:
                act_now.pop(0)()
            h_ = gv(lambda e: e.scalar_tensor_tensor(out=Hs, in0=zh, scalar=0.5, in1=mm, op0=ALU.mult, op1=ALU.add), m_)
            hi_ = gv(lambda e: e.scalar_tensor_tensor(out=new[:, :, 0], in0=c3(zh), scalar=0.5, in1=c3(mm),
                                                      op0=ALU.mult, op1=ALU.add))
            lo_ = gv(lambda e: e.tensor_tensor(new[:, :, 1], c3(Hs), new[:, :, 0], ALU.subtract), hi_)
            state["H"], state["lo"] = h_, lo_
            dst = hb[b % 2][:, :, :, tl * B:tl * B + B].rearrange("p s c n -> p c s n")
            state["kept"] = ga(lambda e: e.activation(dst, new, ACT.Copy), lo_, v_hb_free.get(b - 2))
            if (t + 1) % SUB == 0 and s + 2 < T // SUB:
                load_gi(s + 2, w_)

        v_u_free = [None, None]
        v_x_free = [None] * 3
        v_ah_free = [None] * 3
        v_cb_free = [None]
        v_cmb_free = [None]
        v_d_free = [None] * 4
        turn = [0]
        finished = [-1]

        def fv(fn, *w):
            return f.op("dve", fn, w, "ffn_v")

        def fa(fn, *w):
            return f.op("act", fn, w, "ffn_a")

        def ffn(b, v_h):
            hh = hb[b % 2]

            def mm_(out, l_ap, r_ap, st, sp_, waits, post):
                return f.op("pe", lambda e: e.matmul(out, l_ap, r_ap, start=st, stop=sp_), waits,
                            "ffn_p" if post else None)

            for tc in range(2):
                for c in range(KC):
                    for i, (ph, pw) in enumerate(PROD):
                        st, sp_ = (c == 0 and i == 0), (c == KC - 1 and i == 2)
                        v_lg = mm_(psM[:, tc * 8:tc * 8 + 8], hh[:, ph, c, tc * 128:tc * 128 + 128],
                                   wr_h[:, pw, c * 8:c * 8 + 8], st, sp_,
                                   (v_h, v_cb_free[0], v_small, ("prep_v", f.count["prep_v"])) if st else (), sp_)
                        yield 40.0
            route = {}
            lg = psM[:, 0:16]
            m8, pr, p8, t1, t2 = (rt[:, 16 * k:16 * k + 16] for k in range(5))
            fi, w2, sm = rt[:, 80:96], rt[:, 96:112], rt[:, 112:128]
            pair = lambda a: a.rearrange("p (t e) -> p t e", t=2)
            TC = (slice(0, 8), slice(8, 16))

            def router_1():
                for o in TC:
                    v = fv(lambda e, o=o: e.max(m8[:, o], lg[:, o]), v_lg)
                v = fv(lambda e: e.tensor_scalar(sm[:, 0:2], pair(m8)[:, :, 0], col(C_MIR), None, ALU.mult), v)
                for k, o in enumerate(TC):
                    a = fa(lambda e, k=k, o=o: e.activation(pr[:, o], lg[:, o], ACT.Exp, bias=sm[:, k:k + 1],
                                                            scale=col(C_IR), accum_out=sm[:, 2 + k:3 + k]), v)
                route["a"] = a

            def router_2():
                v = fv(lambda e: e.reciprocal(sm[:, 4:6], sm[:, 2:4]), route["a"])
                for k, o in enumerate(TC):
                    v = fv(lambda e, k=k, o=o: e.tensor_scalar(pr[:, o], pr[:, o], sm[:, 4 + k:5 + k], None, ALU.mult), v)
                for o in TC:
                    vm = fv(lambda e, o=o: e.max(p8[:, o], pr[:, o]), v)
                for o in TC:
                    vi = fv(lambda e, o=o: e.max_index(idx[:, o], p8[:, o], pr[:, o]), vm)
                route["s"] = fv(lambda e: e.tensor_tensor(sm[:, 6:8], pair(p8)[:, :, 0], pair(p8)[:, :, 1], ALU.add), vm)
                route["i"] = fv(lambda e: e.tensor_copy(fi, idx), vi)

            def router_3():
                v = fv(lambda e: e.reciprocal(sm[:, 8:10], sm[:, 6:8]), route["s"])
                for k, o in enumerate(TC):
                    vt = fv(lambda e, k=k, o=o: e.tensor_scalar(t1[:, o], iot, fi[:, 8 * k:8 * k + 1], None, ALU.is_equal),
                            route["i"])
                for k, o in enumerate(TC):
                    vp = fv(lambda e, k=k, o=o: e.tensor_scalar(pr[:, o], pr[:, o], sm[:, 8 + k:9 + k], CB,
                                                                ALU.mult, ALU.mult), v)
                for k, o in enumerate(TC):
                    v = fv(lambda e, k=k, o=o: e.scalar_tensor_tensor(
                        out=t2[:, o], in0=iot, scalar=fi[:, 8 * k + 1:8 * k + 2], in1=t1[:, o],
                        op0=ALU.is_equal, op1=ALU.add), vt, vp)
                v = fv(lambda e: e.tensor_tensor(w2, pr, t2, ALU.mult), v)
                v = fv(lambda e: e.tensor_copy(cmb[:, :, 0], pair(w2)), v, v_cmb_free[0])
                route["v"] = fv(lambda e: e.tensor_tensor(cmb[:, :, 1], pair(w2), cmb[:, :, 0], ALU.subtract), v)

            for r_ in (router_1, router_2, router_3):
                work.append((1000, r_))
            order = list(range(16, 24)) + list(range(16))
            done = {}

            def unit_cb(i):
                e_ = i // 2
                for tc in range(2):
                    for s in range(2):
                        l_ap = cmb[:, tc, s, e_:e_ + 1].broadcast_to([P, 128])
                        last = tc == 1 and s == 1
                        r = mm_(psM[:, 128 * tc:128 * tc + 128], l_ap, idh, s == 0, s == 1,
                                (route["v"], v_cb_free[0]), last)
                        if last:
                            route[e_] = r
                            v_cmb_free[0] = r
                        yield 60.0

            def unit_gu(n_, i):
                k = turn[0] % 2
                if i < 16:
                    cols = ((4 + i // 2, (i % 2) * 128), (4 + i // 2, 256 + (i % 2) * 128))
                else:
                    s = i - 16
                    cols = ((2 * (s // 4), (s % 4) * 128), (2 * (s // 4) + 1, (s % 4) * 128))
                for gu, (e_, o) in enumerate(cols):
                    while e_ not in v_gs:
                        yield None
                    for c in range(KC):
                        for j, (ph, pw) in enumerate(PROD):
                            st, sp_ = (c == 0 and j == 0), (c == KC - 1 and j == 2)
                            w_ap = half(W_GU + e_ * 4 + c, pw)[:, o:o + 128]
                            r = mm_(psU[k][:, 256 * gu:256 * gu + 256], w_ap, hh[:, ph, c, :], st, sp_,
                                    (v_h, v_u_free[k], v_gs[e_], *v_gi_read) if st else (), sp_ and gu == 1)
                            yield 109.0
                return r

            def elementwise(n_, i, r):
                k, x_ = turn[0] % 2, turn[0] % 3
                turn[0] += 1
                t_, a_ = X[x_], AH[x_]
                g, u = psU[k][:, 0:256], psU[k][:, 256:512]
                got = {}

                def gate():
                    got["a"] = fa(lambda e: e.activation(t_, g, ACT.Tanh, scale=col(C_TG)), r, v_x_free[x_],
                                  ("prep_a", f.count["prep_a"]))

                def up():
                    if "a" not in got:
                        gate()
                        act_now.remove(gate)
                    v = fv(lambda e: e.scalar_tensor_tensor(out=t_, in0=t_, scalar=1.0, in1=g,
                                                            op0=ALU.add, op1=ALU.mult), got["a"])
                    if late_dve:
                        late_dve.pop(0)()
                    al = A_RT if i < 16 else A_SH
                    v = fv(lambda e: e.scalar_tensor_tensor(out=t_, in0=t_, scalar=al, in1=u,
                                                            op0=ALU.mult, op1=ALU.mult), v)
                    v_u_free[k] = v
                    if i < 16:
                        v = fv(lambda e: e.tensor_tensor(t_, t_, psM[:, 0:256], ALU.mult), v, route[i // 2])
                        v_cb_free[0] = v
                    got["hi"] = fa(lambda e: e.activation(a_[:, 0], t_, ACT.Copy), v, v_ah_free[x_])
                    late_dve.append(low)

                def low():
                    v = fv(lambda e: e.tensor_tensor(a_[:, 1], t_, a_[:, 0], ALU.subtract), got["hi"])
                    v_x_free[x_] = v
                    done[n_] = (v, x_)

                act_now.append(gate)
                ew.append(up)

            def unit_down(n_, i):
                while n_ not in done or (n_, i) and (i - 16) % 24 not in v_ds:
                    yield None
                v, k = done[n_]
                d_ = (i - 16) % 24
                for hc in range(4):
                    for j, (pa_, pw) in enumerate(PROD):
                        st, sp_ = (n_ == 0 and j == 0), (n_ == 23 and j == 2)
                        w_ap = half(W_D + d_, pw)[:, hc * 128:hc * 128 + 128]
                        r = mm_(psD[hc][:, 0:256], w_ap, AH[k][:, pa_, :], st, sp_,
                                (v, v_ds[d_], v_d_free[hc]) if j == 0 else (), hc == 3 and j == 2)
                        yield 109.0
                v_ah_free[k] = r
                if n_ == 23:
                    def finish():
                        for hc in range(4):
                            v = fv(lambda e, hc=hc: e.scalar_tensor_tensor(
                                out=xy[:, hc, :], in0=psD[hc][:, 0:256], scalar=col(C_OUT), in1=xy[:, hc, :],
                                op0=ALU.mult, op1=ALU.add), r, v_xyl[b])
                            v_d_free[hc] = v
                        v_xys[b] = ld(y[:, 1024 * b:1024 * (b + 1)].rearrange("p (c n) -> p c n", c=KC), xy, "st_y", v)
                        if b + 1 < NBLK:
                            load_xy(b + 1)
                        finished[0] = b

                    work.append((1400, finish))

            for n_, i in enumerate(order):
                r = yield from unit_gu(n_, i)
                if n_ == 23:
                    v_hb_free[b] = r
                if i >= 16:
                    elementwise(n_, i, r)
                if n_ > 1:
                    yield from unit_down(n_ - 2, order[n_ - 2])
                if i < 16:
                    if i % 2 == 0:
                        while "v" not in route or (n_ - 1 not in done and not late_ok(n_ - 1)):
                            yield None
                        yield from unit_cb(i)
                    elementwise(n_, i, r)
            yield from unit_down(22, order[22])
            yield from unit_down(23, order[23])
            while finished[0] != b:
                yield None

        def late_ok(n_):
            return not ew

        def do_work(budget):
            if ew:
                ew.pop(0)()
                budget -= 1700
            elif late_dve:
                late_dve.pop(0)()
                budget -= 500
            while work and budget > 0:
                c, fn = work.pop(0)
                fn()
                budget -= c

        begun = set()
        blocks = []
        current = [None]

        def fill(budget):
            while budget > 0:
                if current[0] is None:
                    if not blocks:
                        return
                    current[0] = blocks.pop(0)
                    begun.add(len(begun) - NBLK + 1)
                c = next(current[0], "end")
                if c == "end":
                    current[0] = None
                    continue
                if c is None:
                    return
                budget -= c

        v_gi_read = []
        for _ in input_gates(0):
            while act_now:
                act_now.pop(0)()
        while act_now:
            act_now.pop(0)()
        load_gi(0, None)
        load_gi(1, None)
        for k in range(PRE_MAX):
            max_gu(k)
        prep_gu()
        blocks += [input_gates(p) for p in range(1, NBLK)]
        downs = False
        for t in range(T):
            while t % TB == 0 and t >= 2 * TB and t // TB - 2 not in v_hb_free:
                fill(2700.0)
                while act_now:
                    act_now.pop(0)()
                do_work(2500.0)
            v_mm = step_pe(t)
            fill(QUOTA if t < TB else (CATCH_UP if t // TB >= 1 and t // TB - 1 not in begun else QUOTA_F))
            step(t, v_mm)
            if not downs and v_d:
                downs = True
                v_gi_read.append(v_ev[12 * NBLK - 1])
                prep_down()
            do_work(WINDOW)
            if (t + 1) % TB == 0:
                blocks.append(ffn(t // TB, state["kept"]))
        while blocks or current[0] is not None or work or ew or late_dve:
            fill(2700.0)
            while act_now:
                act_now.pop(0)()
            do_work(2500.0)

        block = ctx.enter_context(nc.Block())

        @block.sync
        def _(e):
            f.play("sp", e)
            for s in ("st_y", *(f"st_gi{k}" for k in range(8))):
                e.wait_ge(f.sems[s], f.count[s])

        @block.tensor
        def _(e):
            f.play("pe", e)

        @block.vector
        def _(e):
            f.play("dve", e)

        @block.scalar
        def _(e):
            f.play("act", e)


def kernel(x, cond_2048, L0_cond_W_ih, L0_cond_W_hh, L0_cond_b_ih, L0_cond_b_hh, L0_ffn_w_gate,
           L0_ffn_w_gate_up, L0_ffn_w_down, L0_ffn_w_sh_gate_up, L0_ffn_w_sh_down):
    import concourse.bacc as _bacc
    from concourse.bass_utils import run_bass_kernel_spmd as _run

    c = np.ascontiguousarray

    def rows(w):
        k, m = w.shape
        return np.asarray(w).reshape(k // 128, 128, m).transpose(1, 0, 2)

    arrays = {
        "x": c(np.asarray(x).transpose(2, 1, 0).reshape(4, 128, 8, 256).transpose(1, 2, 0, 3).reshape(128, 8192)),
        "h0": c(rows(np.asarray(cond_2048).T).reshape(128, 32)),
        "wih": c(rows(L0_cond_W_ih).reshape(128, 4, 3, 512)[:, :, [0, 2, 1]].reshape(128, 6144)),
        "whh": c(rows(L0_cond_W_hh).reshape(128, 4, 3, 512)[:, :, [0, 2, 1]].reshape(128, 6144)),
        "bih": c(np.asarray(L0_cond_b_ih).reshape(3, 4, 128)[[0, 2, 1]].reshape(12, 128).T),
        "bhh": c(np.asarray(L0_cond_b_hh).reshape(3, 4, 128)[[0, 2, 1]].reshape(12, 128).T),
        "wr": c(rows(L0_ffn_w_gate).reshape(128, 32)),
        "wgu": c(np.concatenate([rows(L0_ffn_w_sh_gate_up).reshape(128, 4, 4, 512)[:, :, [0, 2, 1, 3]].transpose(0, 2, 1, 3),
                                 np.asarray(L0_ffn_w_gate_up).reshape(8, 4, 128, 512).transpose(2, 0, 1, 3)],
                                axis=1).reshape(128, 24576)),
        "wd": c(np.concatenate([rows(L0_ffn_w_sh_down), rows(np.asarray(L0_ffn_w_down).reshape(2048, 512))],
                               axis=1).reshape(128, 12288)),
        "ident": np.eye(128, dtype=np.float32),
        "iota": c(np.broadcast_to(np.arange(8, dtype=np.float32), (128, 8))),
    }
    nc = _bacc.Bacc("TRN2", target_bir_lowering=False, num_devices=1)
    args = [nc.dram_tensor(n, a.shape, mybir.dt.from_np(a.dtype), kind="ExternalInput").ap()
            for n, a in arrays.items()]
    out = nc.dram_tensor("y", (128, 8192), F32, kind="ExternalOutput").ap()
    adaln_ffn(nc, *args, out)
    r = _run(nc, [arrays], core_ids=[0])
    got = r.results[0]["y"]
    return c(got.reshape(128, 8, 4, 32, 8).transpose(4, 1, 3, 2, 0).reshape(8, 256, 512))
```

```python
from contextlib import ExitStack

import numpy as np

import concourse.bass as bass
from concourse import mybir

ALU = mybir.AluOpType
ACT = mybir.ActivationFunctionType
AX = mybir.AxisListType
F32 = mybir.dt.float32
F16 = mybir.dt.float16
U32 = mybir.dt.uint32
U8 = mybir.dt.uint8

P = 128
B, T, D = 8, 256, 512
KC = 4
E = 8
TB = 32
NBLK = T // TB
N = TB * B
SUB = 16
CH = 2048
A_SH = 2.0 ** -64
A_RT = 2.0 ** -74
CB = 1024.0
QUOTA = 3450.0
QUOTA_F = 2980.0
CATCH_UP = 3600.0
WINDOW_0 = 2250.0
WINDOW = 2000.0
WINDOW_A = 2600.0
EARLY = 9
LOAD_STEPS = 4
X_STEPS = 3
X_STEPS_2 = 2
WINDOW_S = 3300.0
NEV = 4
ARENA = 212832
BLOCKS = [(32 * k, 32) for k in range(8)]


class Flow:

    def __init__(self, nc, ctx):
        self.nc, self.ctx = nc, ctx
        self.q = {k: [] for k in ("pe", "dve", "act", "sp")}
        self.count = {}
        self.sems = {}

    def sem(self, name):
        self.sems[name] = self.ctx.enter_context(self.nc.semaphore(name))
        self.count[name] = 0
        return name

    def op(self, eng, fn, waits=(), post=None, by=1):
        if post is not None:
            self.count[post] += by
        self.q[eng].append((tuple(w for w in waits if w is not None), fn, post, by))
        return (post, self.count[post]) if post is not None else None

    def play(self, eng, e):
        met = {}
        for waits, fn, post, by in self.q[eng]:
            need = {}
            for s, v in waits:
                need[s] = max(need.get(s, 0), v)
            for s, v in need.items():
                if met.get(s, 0) < v:
                    e.wait_ge(self.sems[s], v)
                    met[s] = v
            ins = fn(e)
            if post is not None:
                ins.then_inc(self.sems[post], by)


def adaln_ffn(nc, x, h0, wih, whh, bih, bhh, wr, wgu, wd, ident, iota, y):
    with ExitStack() as ctx:
        f = Flow(nc, ctx)

        def psum(name):
            return ctx.enter_context(nc.psum_tensor(name, [P, 512], F32))

        arena = ctx.enter_context(nc.sbuf_tensor("arena", [P, ARENA], U8))
        gi_d = nc.dram_tensor("gi_scratch", [NBLK, P, 12, N], F32)

        def view(off, n, dt):
            size = 2 if dt == F16 else 4
            return arena[:, off:off + n * size].bitcast(dt)

        psG = psum("psG")
        psM = psum("psM")
        psU = [psum("psU0"), psum("psU1")]
        psD = [psum(f"psD{i}") for i in range(4)]

        SHIFT = 2
        W_HH, W_GU, W_D = 0, 12, 60
        W_IH = 72
        X_MAX = W_GU + SHIFT + 16
        D_MAX = W_GU + SHIFT + 32
        U0 = 87 * CH

        def raw(slot, n):
            return view(slot * CH, n * 512, F32)

        def half(slot, part):
            return view(slot * CH + part * 1024, 512, F16)

        gi_2 = view(U0 + 8192, 3072, F32).rearrange("p (s f n) -> p s f n", s=2, f=12)
        hb = [view(U0 + 4096 * k, 2048, F16).rearrange("p (s c n) -> p s c n", s=2, c=KC) for k in range(2)]
        gi = [view(U0 + 8192 + 6144 * k, 1536, F32).rearrange("p (f n) -> p f n", f=12) for k in range(2)]
        xy = view(U0 + 20480, 1024, F32).rearrange("p (c n) -> p c n", c=KC)
        xp_raw = U0 + 20480
        XS = [U0 + 4096, U0 + 24576]
        ev = [view(o, 256, F32) for o in (71 * CH, 71 * CH + 1024, 86 * CH, 86 * CH + 1024)]
        X = [view(o, 256, F32) for o in (U0 + 24576, U0 + 25600, 86 * CH)]
        AH = [view(o, 512, F16).rearrange("p (s n) -> p s n", s=2) for o in (U0 + 26624, U0 + 27648, 86 * CH + 1024)]
        g0 = U0 + 28672
        Tt = view(g0, 576, F32).rearrange("p (f m) -> p f m", f=12)
        g0 += 2304
        Hs, zh, qq, zc, nc1 = [view(g0 + 128 * k, 32, F32) for k in range(5)]
        h0f = qq
        g0 += 640
        Uv = view(g0, 96, F32)
        g0 += 384
        c0 = g0
        idf = view(c0, 128, F32)
        cT = view(c0, 256, F16)
        idh = view(c0 + 512, 128, F16)
        sc = view(c0 + 768, 32, F32)
        iot = view(c0 + 896, 8, F32)
        bi = view(c0 + 928, 12, F32)
        bh = view(c0 + 976, 12, F32)
        bs = view(c0 + 1024, 12, F32)
        wr_h = view(c0 + 1072, 64, F16).rearrange("p (s n) -> p s n", s=2)
        hst = [view(c0 + 1200 + 256 * k, 128, F16).rearrange("p (c q n) -> p c q n", q=4, c=KC) for k in range(2)]
        mx = view(c0 + 1712, 48, F32)
        gcol = view(c0 + 1904, 16, F32)
        rt = view(c0 + 1968, 128, F32)
        wr_raw = rt[:, 0:32]
        cmb = view(c0 + 2480, 32, F16).rearrange("p (t s e) -> p t s e", t=2, s=2)
        idx = view(c0 + 2544, 16, U32)
        sel = view(c0 + 2608, 8, F16)
        assert c0 + 2624 <= ARENA

        for n_ in ("ld_i", "ld_a", "ld_x0", "ld_x1", "ld_ih0", "ld_ih1", "ld_hh0", "ld_hh1", "ld_e0", "ld_e1", "ld_l0", "ld_l1",
                   *(f"ld_gu{q}" for q in range(6)), *(f"ld_d{q}" for q in range(3)), "ld_gi0",
                   "ld_gi1", "ld_xy", "ld_xp", "st_y", "prep_v", "prep_a", "prep_p", "gi_p", "gi_a",
                   "gru_p", "gru_v", "gru_a", "ffn_p", "ffn_v", "ffn_a"):
            f.sem(n_)
        for k in range(NEV):
            f.sem(f"st_gi{k}")

        def ld(out, in_, post, *waits):
            return f.op("sp", lambda e: e.dma_start(out, in_), waits, post, 16)

        def pv(fn, *waits):
            return f.op("dve", fn, waits, "prep_v")

        def pa(fn, *waits):
            return f.op("act", fn, waits, "prep_a")

        def col(k):
            return sc[:, k:k + 1]

        (PX0, PIH, PHH, PR, PH, PX1, PX, PGU, PD) = range(9)
        SX0, SIH, SHH, SR, SH_, SX1, SX, SGU, SD = range(10, 19)
        (C_SH, C_TR, C_TN, C_GI0, C_GI1, C_GI, C_IR, C_MIR, C_TG, C_OUT, C_T0, C_T1) = range(20, 32)

        def piece(w, dst, first, n, sem, *waits):
            return ld(raw(dst, n), w[:, 512 * first:512 * (first + n)], sem, *waits)

        v_xp, v_xs, v_gi_piece, v_st = {}, {}, {}, {}
        now, at = [-X_STEPS], {}

        def load_xp(p):
            at[("x", p)] = now[0] if p == 1 else now[0] + (X_STEPS if now[0] < 8 else X_STEPS_2)
            v_xp[p] = ld(view(xp_raw, 1024, F32), x[:, 1024 * p:1024 * (p + 1)], "ld_xp", v_xs.get(p - 1))

        v_i = ld(idf, ident, "ld_i")
        load_xp(0)
        v_ihl = [piece(wih, W_IH + SHIFT + 6 * q, 6 * q, 6, f"ld_ih{q}") for q in range(2)]
        v_hhl = [piece(whh, W_HH + SHIFT + 6 * q, 6 * q, 6, f"ld_hh{q}") for q in range(2)]
        for out, src in ((h0f, h0), (wr_raw, wr), (iot, iota), (bi, bih), (bh, bhh)):
            v_a = ld(out, src, "ld_a")

        def rowmax(out, in_, *waits):
            return pv(lambda e: e.tensor_reduce(out, in_, AX.X, ALU.max, apply_absolute_value=True), *waits)

        def rowsum(out, in_, *waits):
            return pa(lambda e: e.activation(in_, in_, ACT.Abs, accum_out=out), *waits)

        def spread(k0, nk, *dep):
            v = f.op("pe", lambda e: e.matmul(psM[0:nk, 0:128], gcol[:, k0:k0 + nk], idf[:, :], start=True, stop=True),
                     (*dep, v_i), "prep_p")
            v = pv(lambda e: e.tensor_reduce(mx[0:nk, 40:41], psM[0:nk, 0:128], AX.X, ALU.max), v)
            v = f.op("pe", lambda e: e.matmul(psM[:, 0:nk], mx[0:nk, 40:41].broadcast_to([nk, 128]), idf[0:nk, 0:nk],
                                              start=True, stop=True), (v,), "prep_p")
            return pv(lambda e: e.tensor_scalar(sc[:, k0:k0 + nk], psM[:, 0:nk], 2.0 ** -40, None, ALU.max), v)

        def floors(k0, nk, v):
            bits = sc[:, k0:k0 + nk].bitcast(U32)
            v = pv(lambda e: e.tensor_scalar(bits, bits, 0x7F800000, None, ALU.bitwise_and), v)
            v = pv(lambda e: e.reciprocal(sc[:, 10 + k0:10 + k0 + nk], sc[:, k0:k0 + nk]), v)
            return pv(lambda e: e.tensor_scalar(sc[:, 10 + k0:10 + k0 + nk], sc[:, 10 + k0:10 + k0 + nk],
                                                2.0 ** 14, None, ALU.mult), v)

        def prod(out, a, b, k, v):
            return pv(lambda e: e.scalar_tensor_tensor(out=col(out), in0=col(a), scalar=k, in1=col(b),
                                                       op0=ALU.mult, op1=ALU.mult), v)

        v_z = [pv(lambda e, k=k: e.memset(hst[k], 0.0)) for k in range(2)][-1]
        rowmax(gcol[:, PX0:PX0 + 1], view(xp_raw, 1024, F32), v_xp[0])
        rowmax(mx[:, 41:42], raw(W_IH + SHIFT, 6), v_ihl[0])
        v_ihm = pa(lambda e: e.activation(raw(W_D + 1, 3), raw(W_IH + SHIFT + 9, 3), ACT.Abs, accum_out=mx[:, 42:43]), v_ihl[1])
        v = rowmax(mx[:, 43:44], raw(W_IH + SHIFT + 6, 3), v_ihl[1])
        v = rowmax(gcol[:, PIH:PIH + 1], mx[:, 41:44], v, v_ihm)
        v = spread(PX0, 2, v)
        v_sc = floors(PX0, 2, v)

        def split(src, hi, lo, scale, *waits):
            v = pa(lambda e: e.activation(hi, src, ACT.Copy, scale=scale), *waits)
            return pv(lambda e: e.scalar_tensor_tensor(out=lo, in0=src, scalar=scale, in1=hi,
                                                       op0=ALU.mult, op1=ALU.subtract), v)

        def split_row(base, n, scale, dep, v):
            old = [v] * SHIFT
            for k in range(n):
                old.append(split(raw(base + SHIFT + k, 1), half(base + k, 0), half(base + k, 1), scale, dep(k), old[k]))
                yield old[-1]

        def x_raw(k):
            return view(xp_raw + CH * k, 512, F32)

        def x_half(p, k, part):
            return view(XS[p % 2] + CH * k + 1024 * part, 512, F16)

        for k in range(2):
            v_xs[0] = split(x_raw(k), x_half(0, k, 0), x_half(0, k, 1), col(SX0), v_xp[0], v_sc)
        load_xp(1)
        v_xl = [piece(x, X_MAX + 6 * q, 4 + 6 * q, 6, f"ld_x{q}") for q in range(2)]
        ih_split = split_row(W_IH, 12, col(SIH), lambda k: v_ihl[k // 6], v_sc)
        v_ihs = {k: next(ih_split) for k in range(8)}
        v_late = [piece(wd, D_MAX + 8 * q, EARLY + 8 * q, (8, 7)[q], f"ld_l{q}") for q in range(2)]
        v_gu = {q: piece(wgu, W_GU + SHIFT + 8 * q, 8 * q, 8, f"ld_gu{q}") for q in range(2)}
        v_t0 = prod(C_T0, PX0, PIH, 2.0 ** -28, v_sc)
        v_bias = {}
        c3 = lambda a: a.rearrange("p (c b) -> p c b", b=B)

        class Splits:

            def __init__(self, n, aps, scale, dep, start, done):
                self.n, self.aps, self.scale, self.dep, self.done = n, aps, scale, dep, done
                self.low = [start] * SHIFT
                self.high = []

            def ahead(self):
                k = len(self.high)
                if k < self.n and k < len(self.low) and self.dep(k) is not None:
                    src, hi, _ = self.aps(k)
                    self.high.append(pa(lambda e: e.activation(hi, src, ACT.Copy, scale=self.scale),
                                        *self.dep(k), self.low[k]))
                    return True

            def follow(self):
                k = len(self.low) - SHIFT
                src, hi, lo = self.aps(k)
                self.low.append(pv(lambda e: e.scalar_tensor_tensor(out=lo, in0=src, scalar=self.scale, in1=hi,
                                                                    op0=ALU.mult, op1=ALU.subtract), self.high[k]))
                self.done(k, self.low[-1])

            def ready(self):
                return len(self.low) - SHIFT < len(self.high)

            def over(self):
                return len(self.low) - SHIFT == self.n

        def in_place(base):
            return lambda k: (raw(base + SHIFT + k, 1), half(base + k, 0), half(base + k, 1))

        PROD = ((0, 0), (0, 1), (1, 0))

        act_now = []
        late_dve = []
        ew = []
        work = []
        act_work = []
        urgent = []

        gi_ps = [psU[0], psU[1], *psD]
        v_ev, v_evs, made = {}, {}, []

        def input_gates(p):
            while p not in v_xs:
                yield None
            for fc in range(12):
                n = 12 * p + fc
                ps = gi_ps[n % 6][:, 0:N]
                while n >= 6 and n - 6 not in v_ev:
                    yield None
                for c in range(KC):
                    for i, (px, pw) in enumerate(PROD):
                        w_ap = half(W_IH + fc // 4 * 4 + c, pw)[:, (fc % 4) * 128:(fc % 4) * 128 + 128]
                        x_ap = x_half(p, c // 2, px)[:, (c % 2) * 256:(c % 2) * 256 + 256]
                        st, sp_ = (c == 0 and i == 0), (c == KC - 1 and i == 2)
                        r = f.op("pe", lambda e, ps=ps, w_ap=w_ap, x_ap=x_ap, st=st, sp_=sp_:
                                 e.matmul(ps, w_ap, x_ap, start=st, stop=sp_),
                                 (v_ihs[fc // 4 * 4 + 3], v_xs[p], v_ev.get(n - 6)) if st else (), "gi_p" if sp_ else None)
                        yield 109.0

                def evacuate(n=n, fc=fc, ps=ps, r=r):
                    if p == 0:
                        o_ap, i_ap, free = gi_2[:, :, fc], ps.rearrange("p (s n) -> p s n", s=2), None
                    else:
                        o_ap, i_ap, free = ev[n % NEV], ps, v_evs.get(n - NEV)
                    cg = col((C_GI0, C_GI1, C_GI)[min(p, 2)])
                    if p == 0 and fc % 2:
                        v_ev[n] = pv(lambda e: e.tensor_scalar(o_ap, i_ap, cg, bs[:, fc:fc + 1], ALU.mult, ALU.add),
                                     r, v_bias[0])
                    else:
                        v_ev[n] = f.op("act", lambda e: e.activation(o_ap, i_ap, ACT.Identity, bias=bs[:, fc:fc + 1],
                                                                     scale=cg), (r, v_bias[min(p, 2)], free), "gi_a")
                    if p:
                        v_evs[n] = ld(gi_d[p, :, fc, :], ev[n % NEV], f"st_gi{n % NEV}", v_ev[n])
                        v_st.setdefault(p, []).append(v_evs[n])

                act_now.append(evacuate)
                made.append(n)
            v_gi_piece[p] = r
            if p + 2 < NBLK:
                split_x(p + 2)
            if p == NBLK - 1:
                while len(v_st.get(p, ())) < 12:
                    yield None
                stored = [w for q in v_st.values() for w in q]
                v_gi_read.extend((v_ev[12 * NBLK - 1], r, *stored[-4:]))
                while not v_gus:
                    yield None
                for q in range(3):
                    at[("d", q)] = now[0] + 2 + q
                    v_d[q] = piece(wd, W_D + SHIFT + EARLY + 5 * q, EARLY + 5 * q, 5, f"ld_d{q}", r, *v_gus, *stored)
                load_xy(0)

        v_d, v_gus, v_gs, v_ds = {}, [], {}, {}
        v_gil, v_xyl, v_xys = {}, {}, {}

        def load_gi(s, free):
            off = (s * SUB * B) % N
            p = (s * SUB * B) // N
            assert len(v_st[p]) == 12
            v_gil[s] = ld(gi[s % 2], gi_d[p, :, :, off:off + SUB * B], f"ld_gi{s % 2}", *v_st[p], free)

        def load_xy(b):
            v_xyl[b] = ld(xy[:, :, 0:BLOCKS[b][1] * B], of_tokens(x, b), "ld_xy", v_xys.get(b - 1, v_xs[NBLK - 1]))

        def of_tokens(a, b):
            t0, nt = BLOCKS[b]
            q, o = t0 // TB, (t0 % TB) * B
            return a[:, 1024 * q:1024 * (q + 1)].rearrange("p (c n) -> p c n", c=KC)[:, :, o:o + nt * B]

        splits = []
        junk = raw(W_GU, 2)
        bounds, v_xsums, v_sums, v_maxs, v_sx = [], [], [], [], []
        v_early = []
        scaled = []

        def split_x(p):
            def done(k, v):
                if k == 1:
                    v_xs[p] = v
                    if p + 1 < NBLK:
                        load_xp(p + 1)

            def dep(k):
                if p in v_xp and (p == 1 or v_sx) and now[0] >= at[("x", p)]:
                    return (v_xp[p], v_s2) if p == 1 else (v_xp[p], v_sx[0], v_gi_piece[p - 2])

            splits.insert(0, Splits(2, lambda k: (x_raw(k), x_half(p, k, 0), x_half(p, k, 1)), col(SX1 if p == 1 else SX),
                                    dep, None, done))

        def sum_x(k):
            v_xsums.append(pa(lambda e: e.activation(raw(X_MAX + 2 * k, 2), raw(X_MAX + 2 * k, 2), ACT.Abs,
                                                     accum_out=gcol[:, 10 + k:11 + k]), v_xl[k // 3]))
            if k == 5:
                stages(PX, (gcol[:, 10:16],), then_x, 0)

        def then_x(v):
            v_sx.append(v)
            v = prod(C_T0, PX, PIH, 2.0 ** -28, v)
            v_bias[2] = prod(C_GI, C_T0, C_SH, 1.0, v)

        def bound(k, of, *waits):
            v_sums.append(pa(lambda e: e.activation(junk[:, 0:of.shape[-1]], of, ACT.Abs, accum_out=mx[:, k:k + 1]),
                             v_sums[-1] if v_sums else v_hhs[0], *waits))
            bounded(k)

        def bounded(k):
            bounds.append(k)
            if len(bounds) == 37:
                scales()

        def stages(k0, cols, then, place):
            got, nk = {}, len(cols)

            def s1():
                for k, c in enumerate(cols):
                    v = rowmax(gcol[:, k0 + k:k0 + k + 1], c, *(q[-1] for q in (v_xsums, v_sums, v_maxs) if q))
                got["p"] = f.op("pe", lambda e: e.matmul(psM[0:nk, 0:128], gcol[:, k0:k0 + nk], idf[:, :],
                                                         start=True, stop=True), (v, v_i), "prep_p")

            def s2():
                v = pv(lambda e: e.tensor_reduce(mx[0:nk, 40:41], psM[0:nk, 0:128], AX.X, ALU.max), got["p"])
                got["p"] = f.op("pe", lambda e: e.matmul(psM[:, 0:nk], mx[0:nk, 40:41].broadcast_to([nk, 128]),
                                                         idf[0:nk, 0:nk], start=True, stop=True), (v,), "prep_p")

            def s3():
                v = pv(lambda e: e.tensor_scalar(sc[:, k0:k0 + nk], psM[:, 0:nk], 2.0 ** -40, None, ALU.max), got["p"])
                then(floors(k0, nk, v))

            work[place:place] = [(300, s1), (300, s2), (1200, s3)]

        def scales():
            def done(k, v):
                if k % 4 == 3:
                    v_gs[k // 4] = v
                if k == 47:
                    v_gus.append(v)

            def then(v0):
                v = prod(C_TG, PGU, PH, 2.0 ** -29, v0)
                splits.append(Splits(48, in_place(W_GU), col(SGU), lambda k: (v_gu[k // 8],), v, done))
                v = prod(C_T0, PGU, PH, 2.0 ** 3, v0)
                v = prod(C_T1, C_T0, C_T0, 1.0, v)
                v = prod(C_OUT, PD, C_T1, 2.0 ** -13, v)
                scaled.append(v)
                splits.append(Splits(24, in_place(W_D), col(SD), of_d, v, v_ds.__setitem__))

            def of_d(k):
                if v_gus and (k < EARLY or v_d and now[0] >= at[("d", (k - EARLY) // 5)]):
                    return v_gus[0], v_early[k // 5] if k < EARLY else v_d[(k - EARLY) // 5]

            stages(PGU, (mx[:, 0:24], mx[:, 24:37]), then, len(work))

        gv = lambda fn, *w: f.op("dve", fn, w, "gru_v")
        ga = lambda fn, *w: f.op("act", fn, w, "gru_a")
        whv = [[view((W_HH + c * 3) * CH, 3 * 1024, F16)
                .rearrange("p (g s c k) -> p g s c k", g=3, s=2, c=KC)[:, :, part] for part in range(2)]
               for c in range(KC)]
        v_hb_free = {}
        block_of = [b for b, (t0, n) in enumerate(BLOCKS) for _ in range(n)]
        Tin = Tt.rearrange("p f (i m) -> p f m i", i=3)
        U3 = c3(Uv)
        Ur, Uz, Un = Uv[:, 0:32], Uv[:, 32:64], Uv[:, 64:96]

        def gt_of(t):
            return gi[t // SUB % 2][:, :, (t % SUB) * B:(t % SUB) * B + B]

        def place_gates(t, *waits):
            return ga(lambda e: e.activation(Tt[:, 0:8, 32:40], gt_of(t)[:, 0:8], ACT.Copy), v_gil[t // SUB], *waits)

        def step_pe(t):
            prev = hst[(t + 1) % 2]
            first = True
            for c in range(KC):
                for part in range(2):
                    for j in range(4):
                        w_ap = whv[c][part][:, :, :, 32 * j:32 * j + 32]
                        l_ap = prev[:, c].rearrange("p q n -> p (q n)")
                        o_ap = psG[32 * j:32 * j + 32, 0:384]
                        fin = c == KC - 1 and part == 1 and j == 3
                        r = f.op("pe", lambda e, o_ap=o_ap, l_ap=l_ap, w_ap=w_ap, c=c, part=part, j=j:
                                 e.matmul(o_ap, l_ap, w_ap, start=(c == 0 and part == 0), stop=(c == KC - 1 and part == 1),
                                          tile_position=(0, 32 * j)),
                                 (state["lo"], v_hhs[0]) if first else (), "gru_p" if fin else None)
                        first = False
            return r

        def step(t, v_mm):
            b = block_of[t]
            tl = t - BLOCKS[b][0]
            s = t // SUB
            gt = gt_of(t)
            new = hst[t % 2]
            t_r = gv(lambda e: e.transpose(Tt[:, 0:4, 0:32], psG[:, 0:128].rearrange("p (f m) -> p f m", m=32)), v_mm)
            t_zn = gv(lambda e: e.transpose(Tt[:, 4:12, 0:32], psG[:, 128:384].rearrange("p (f m) -> p f m", m=32)),
                      state["placed"])
            r_r = gv(lambda e: e.tensor_reduce(U3[:, 0:4], Tin[:, 0:4, 0:B], AX.X, ALU.add), t_r)
            s_r = ga(lambda e: e.activation(Ur, Ur, ACT.Tanh, scale=col(C_TR)), r_r)
            r_zn = gv(lambda e: e.tensor_reduce(U3[:, 4:12], Tin[:, 4:12, 0:B], AX.X, ALU.add), t_zn)
            s_z = ga(lambda e: e.activation(Uz, Uz, ACT.Tanh, scale=col(C_TR)), r_zn)
            q_ = gv(lambda e: e.scalar_tensor_tensor(out=qq, in0=Ur, scalar=1.0, in1=Un, op0=ALU.add, op1=ALU.mult),
                    s_r, r_zn)
            w_ = gv(lambda e: e.scalar_tensor_tensor(out=c3(qq), in0=c3(qq), scalar=0.5, in1=gt[:, 8:12, :],
                                                     op0=ALU.mult, op1=ALU.add), q_)
            s_n = ga(lambda e: e.activation(qq, qq, ACT.Tanh, scale=col(C_TN)), w_)
            zc_ = gv(lambda e: e.scalar_tensor_tensor(out=zc, in0=Uz, scalar=-1.0, in1=nc1, op0=ALU.add, op1=ALU.mult),
                     s_z)
            zh_ = gv(lambda e: e.scalar_tensor_tensor(out=zh, in0=Uz, scalar=1.0, in1=Hs, op0=ALU.add, op1=ALU.mult),
                     state["H"])
            m_ = gv(lambda e: e.tensor_tensor(zc, zc, qq, ALU.mult), s_n, zc_)
            if t + 1 < T:
                state["placed"] = place_gates(t + 1)
            while act_now:
                act_now.pop(0)()
            h_ = gv(lambda e: e.scalar_tensor_tensor(out=Hs, in0=zh, scalar=0.5, in1=zc, op0=ALU.mult, op1=ALU.add), m_)
            hi_ = gv(lambda e: e.scalar_tensor_tensor(out=new[:, :, 0], in0=c3(zh), scalar=0.5, in1=c3(zc),
                                                      op0=ALU.mult, op1=ALU.add))
            lo_ = gv(lambda e: e.tensor_tensor(new[:, :, 2], c3(Hs), new[:, :, 0], ALU.subtract), hi_)
            state["H"], state["lo"] = h_, lo_
            dst = hb[b % 2][:, :, :, tl * B:tl * B + B].rearrange("p s c n -> p c s n")
            src = new.rearrange("p c (s z) n -> p c s z n", s=2)[:, :, :, 0]
            free = v_gi_piece[NBLK - 2] if b == 1 else v_hb_free.get(b - 2)
            state["kept"] = ga(lambda e: e.activation(dst, src, ACT.Copy), lo_, free)
            if (t + 1) % SUB == 0 and s + 2 < T // SUB:
                load_gi(s + 2, w_)

        v_u_free = [None, None]
        v_x_free = [None] * 3
        v_ah_free = [None] * 3
        v_cb_free = [None]
        v_cmb_free = [None]
        v_d_free = [None] * 4
        turn = [0]
        current_nt = [N]
        gone = [0]
        finished = [-1]
        downs = [0]
        begun = set()

        def fv(fn, *w):
            return f.op("dve", fn, w, "ffn_v")

        def fa(fn, *w):
            return f.op("act", fn, w, "ffn_a")

        def ffn(b, v_h):
            t0, nt = BLOCKS[b][0], BLOCKS[b][1] * B
            ntc = nt // 128
            hh = hb[b % 2]
            current_nt[0] = nt

            def mm_(out, l_ap, r_ap, st, sp_, waits, post):
                return f.op("pe", lambda e: e.matmul(out, l_ap, r_ap, start=st, stop=sp_), waits,
                            "ffn_p" if post else None)

            route = {}
            lg = psM[:, 0:8 * ntc]
            m8, pr, p8, t1, t2 = (rt[:, 16 * k:16 * k + 8 * ntc] for k in range(5))
            fi, w2, sm = rt[:, 80:80 + 8 * ntc], rt[:, 96:96 + 8 * ntc], rt[:, 112:128]
            pair = lambda a: a.rearrange("p (t e) -> p t e", e=E)
            ix = idx[:, 0:8 * ntc]
            TC = (slice(0, 8), slice(8, 16))[:ntc]

            def router_1():
                for o in TC:
                    v = fv(lambda e, o=o: e.max(m8[:, o], lg[:, o]), route["l"])
                v = fv(lambda e: e.tensor_scalar(sm[:, 0:ntc], pair(m8)[:, :, 0], col(C_MIR), None, ALU.mult), v)
                for k, o in enumerate(TC):
                    a = fa(lambda e, k=k, o=o: e.activation(pr[:, o], lg[:, o], ACT.Exp, bias=sm[:, k:k + 1],
                                                            scale=col(C_IR), accum_out=sm[:, 2 + k:3 + k]), v)
                route["a"] = a

            def router_2():
                v = fv(lambda e: e.reciprocal(sm[:, 4:4 + ntc], sm[:, 2:2 + ntc]), route["a"])
                for k, o in enumerate(TC):
                    v = fv(lambda e, k=k, o=o: e.tensor_scalar(pr[:, o], pr[:, o], sm[:, 4 + k:5 + k], None, ALU.mult), v)
                for o in TC:
                    vm = fv(lambda e, o=o: e.max(p8[:, o], pr[:, o]), v)
                for o in TC:
                    vi = fv(lambda e, o=o: e.max_index(ix[:, o], p8[:, o], pr[:, o]), vm)
                route["s"] = fv(lambda e: e.tensor_tensor(sm[:, 6:6 + ntc], pair(p8)[:, :, 0], pair(p8)[:, :, 1], ALU.add), vm)
                route["i"] = fv(lambda e: e.tensor_copy(fi, ix), vi)

            def router_3():
                v = fv(lambda e: e.reciprocal(sm[:, 8:8 + ntc], sm[:, 6:6 + ntc]), route["s"])
                for k, o in enumerate(TC):
                    vt = fv(lambda e, k=k, o=o: e.tensor_scalar(t1[:, o], iot, fi[:, 8 * k:8 * k + 1], None, ALU.is_equal),
                            route["i"])
                for k, o in enumerate(TC):
                    vp = fv(lambda e, k=k, o=o: e.tensor_scalar(pr[:, o], pr[:, o], sm[:, 8 + k:9 + k], CB,
                                                                ALU.mult, ALU.mult), v)
                for k, o in enumerate(TC):
                    v = fv(lambda e, k=k, o=o: e.scalar_tensor_tensor(
                        out=t2[:, o], in0=iot, scalar=fi[:, 8 * k + 1:8 * k + 2], in1=t1[:, o],
                        op0=ALU.is_equal, op1=ALU.add), vt, vp)
                v = fv(lambda e: e.tensor_tensor(w2, pr, t2, ALU.mult), v)
                v = fv(lambda e: e.tensor_copy(cmb[:, 0:ntc, 0], pair(w2)), v, v_cmb_free[0])
                route["v"] = fv(lambda e: e.tensor_tensor(cmb[:, 0:ntc, 1], pair(w2), cmb[:, 0:ntc, 0], ALU.subtract), v)

            def logits():
                for tc in range(ntc):
                    for c in range(KC):
                        for i, (ph, pw) in enumerate(PROD):
                            st, sp_ = (c == 0 and i == 0), (c == KC - 1 and i == 2)
                            route["l"] = mm_(psM[:, tc * 8:tc * 8 + 8], hh[:, ph, c, tc * 128:tc * 128 + 128],
                                       wr_h[:, pw, c * 8:c * 8 + 8], st, sp_,
                                       (v_h, v_cb_free[0], v_small, ("prep_v", f.count["prep_v"])) if st else (), sp_)
                            yield 40.0
                for r_ in (router_1, router_2, router_3):
                    work.append((1000, r_))

            order = list(range(16, 24)) + list(range(16))
            done = {}

            def unit_ct():
                for tc in range(ntc):
                    r = mm_(psM[0:16, 128 * tc:128 * tc + 128], cmb[:, tc].rearrange("p s e -> p (s e)"), idh, True, True,
                            (route["v"], v_cb_free[0]), tc == ntc - 1)
                    yield 60.0
                v_cmb_free[0] = r

                def keep():
                    route["t"] = fa(lambda e: e.activation(cT[0:16, 0:nt], psM[0:16, 0:nt], ACT.Copy), r)

                act_now.append(keep)

            def unit_cb(i):
                while "t" not in route:
                    yield None
                e_ = i // 2
                route[e_] = mm_(psM[:, 0:nt], sel[0:16, e_:e_ + 1].broadcast_to([16, 128]), cT[0:16, 0:nt], True, True,
                                (route["t"], v_cb_free[0]), True)
                yield nt / 2.4 + 2.5

            def unit_gu(n_, i):
                k = turn[0] % 2
                while turn[0] - 2 >= gone[0]:
                    yield None
                if i < 16:
                    cols = ((4 + i // 2, (i % 2) * 128), (4 + i // 2, 256 + (i % 2) * 128))
                else:
                    s = i - 16
                    cols = ((2 * (s // 4), (s % 4) * 128), (2 * (s // 4) + 1, (s % 4) * 128))
                for gu, (e_, o) in enumerate(cols):
                    while e_ not in v_gs:
                        yield None
                    for c in range(KC):
                        for j, (ph, pw) in enumerate(PROD):
                            st, sp_ = (c == 0 and j == 0), (c == KC - 1 and j == 2)
                            w_ap = half(W_GU + e_ * 4 + c, pw)[:, o:o + 128]
                            r = mm_(psU[k][:, 256 * gu:256 * gu + nt], w_ap, hh[:, ph, c, 0:nt], st, sp_,
                                    (v_h, v_u_free[k], v_gs[e_], *v_gi_read) if st else (), sp_ and gu == 1)
                            yield nt / 2.4 + 2.5
                return r

            def elementwise(n_, i, r):
                k, x_ = turn[0] % 2, turn[0] % 3
                turn[0] += 1
                t_, a_ = X[x_][:, 0:nt], AH[x_][:, :, 0:nt]
                g, u = psU[k][:, 0:nt], psU[k][:, 256:256 + nt]
                got = {}

                def gate():
                    got["a"] = fa(lambda e: e.activation(t_, g, ACT.Tanh, scale=col(C_TG)), r, v_x_free[x_], *v_gi_read)

                def up():
                    if "a" not in got:
                        gate()
                        act_now.remove(gate)
                    v = fv(lambda e: e.scalar_tensor_tensor(out=t_, in0=t_, scalar=1.0, in1=g,
                                                            op0=ALU.add, op1=ALU.mult), got["a"])
                    if late_dve:
                        late_dve.pop(0)()
                    al = A_RT if i < 16 else A_SH
                    v = fv(lambda e: e.scalar_tensor_tensor(out=t_, in0=t_, scalar=al, in1=u,
                                                            op0=ALU.mult, op1=ALU.mult), v)
                    v_u_free[k] = v
                    gone[0] += 1
                    if i < 16:
                        v = fv(lambda e: e.tensor_tensor(t_, t_, psM[:, 0:nt], ALU.mult), v, route[i // 2])
                        v_cb_free[0] = v
                    got["hi"] = fa(lambda e: e.activation(a_[:, 0], t_, ACT.Copy), v, v_ah_free[x_])
                    late_dve.append(low)

                def low():
                    v = fv(lambda e: e.tensor_tensor(a_[:, 1], t_, a_[:, 0], ALU.subtract), got["hi"])
                    v_x_free[x_] = v
                    done[n_] = (v, x_)

                act_now.append(gate)
                ew.append((1700 if nt == N else 1000, up))

            def unit_down(n_, i):
                while n_ not in done or (i - 16) % 24 not in v_ds:
                    yield None
                v, k = done[n_]
                d_ = (i - 16) % 24
                for hc in range(4):
                    for j, (pa_, pw) in enumerate(PROD):
                        st, sp_ = (n_ == 0 and j == 0), (n_ == 23 and j == 2)
                        w_ap = half(W_D + d_, pw)[:, hc * 128:hc * 128 + 128]
                        r = mm_(psD[hc][:, 0:nt], w_ap, AH[k][:, pa_, 0:nt], st, sp_,
                                (v, v_ds[d_], v_d_free[hc]) if j == 0 else (), hc == 3 and j == 2)
                        yield nt / 2.4 + 2.5
                v_ah_free[k] = r
                downs[0] += 1
                if n_ == 23:
                    def finish(hc):
                        v = fv(lambda e: e.scalar_tensor_tensor(
                            out=xy[:, hc, 0:nt], in0=psD[hc][:, 0:nt], scalar=col(C_OUT), in1=xy[:, hc, 0:nt],
                            op0=ALU.mult, op1=ALU.add), r, v_xyl[b])
                        v_d_free[hc] = v
                        if hc == 3:
                            v_xys[b] = ld(of_tokens(y, b), xy[:, :, 0:nt], "st_y", v)
                            if b + 1 < len(BLOCKS):
                                load_xy(b + 1)
                            finished[0] = b

                    urgent.extend((350, lambda hc=hc: finish(hc)) for hc in range(4))

            started = turn[0]
            while b == 0 and not v_gi_read:
                yield None
            begun.add(b)
            for n_, i in enumerate(order):
                if n_ == 1:
                    while gone[0] < started or not scaled:
                        yield None
                    yield from logits()
                if n_ > 3 and "v" in route and "c" not in route:
                    route["c"] = True
                    yield from unit_ct()
                r = yield from unit_gu(n_, i)
                if n_ == 23:
                    v_hb_free[b] = r
                while downs[0] < turn[0] - 2:
                    yield None
                if i >= 16:
                    elementwise(n_, i, r)
                if n_ > 1:
                    while finished[0] != b - 1:
                        yield None
                    yield from unit_down(n_ - 2, order[n_ - 2])
                if i < 16:
                    if i % 2 == 0:
                        while "c" not in route and "v" not in route:
                            yield None
                        if "c" not in route:
                            route["c"] = True
                            yield from unit_ct()
                        while n_ - 1 not in done and ew:
                            yield None
                        yield from unit_cb(i)
                    elementwise(n_, i, r)
            yield from unit_down(22, order[22])
            yield from unit_down(23, order[23])

        def do_work(budget, a_budget=WINDOW_A):
            def spend(queue, n):
                left = budget
                while queue and left > 0 and n > 0:
                    c, fn = queue.pop(0)
                    fn()
                    left -= c
                    n -= 1
                    if fn.__name__ in ("s1", "s2"):
                        break
                return left

            budget = spend(urgent, 4)
            if not ew and late_dve:
                late_dve.pop(0)()
                budget -= 500
            budget = spend(ew, 1)
            for q in splits:
                while q.ready() and budget > 0:
                    q.follow()
                    q.ahead()
                    budget -= 700
                    a_budget -= 560
            splits[:] = [q for q in splits if not q.over()]
            budget = spend(work, 9)
            spend(ew, 1)
            for q in splits:
                while q.ahead():
                    a_budget -= 560
            while act_work and a_budget > 0:
                c, fn = act_work.pop(0)
                fn()
                a_budget -= c

        blocks = []

        def fill(budget):
            while budget > 0:
                for g in blocks[:2]:
                    c = next(g, "end")
                    if c == "end":
                        blocks.remove(g)
                        break
                    if c is not None:
                        budget -= c
                        break
                else:
                    return

        v_gi_read = []
        x_sums, v_hhs = [], []
        gates_0 = input_gates(0)

        def next_gates(k):
            for _ in gates_0:
                if len(made) > k:
                    break

        for k in range(4):
            next_gates(k)
        rowmax(gcol[:, PR:PR + 1], wr_raw, v_a)
        rowmax(gcol[:, PH:PH + 1], h0f, v_a)
        v = rowmax(mx[:, 44:45], raw(W_HH + SHIFT, 3), v_hhl[0])
        v_hm = pa(lambda e: e.activation(raw(W_D + 1, 9), raw(W_HH + SHIFT + 3, 9), ACT.Abs, accum_out=mx[:, 45:46]),
                  *v_hhl, v_ihm)
        v = rowmax(gcol[:, PHH:PHH + 1], mx[:, 44:46], v, v_hm)
        for k in range(3):
            sum_x(k)
        v = rowmax(gcol[:, PX1:PX1 + 1], view(xp_raw, 1024, F32), v_xp[1])
        v = spread(PHH, 4, v)
        v = pv(lambda e: e.tensor_scalar(col(PH), col(PH), 1.0, None, ALU.max), v)
        v_s2 = v = floors(PHH, 4, v)
        v_cs = prod(C_SH, SHH, SH_, 1.0, v)
        v_tn = prod(C_TN, PHH, PH, 2.0 ** -28, v)
        v = pv(lambda e: e.tensor_tensor(bs[:, 0:8], bi[:, 0:8], bh[:, 0:8], ALU.add), v_a)
        v = pv(lambda e: e.tensor_copy(bs[:, 8:12], bi[:, 8:12]), v_a)
        v = pv(lambda e: e.tensor_scalar(bs, bs, col(C_SH), None, ALU.mult), v_cs, v)
        v_bias[0] = prod(C_GI0, C_T0, C_SH, 1.0, v_cs)
        h03 = c3(h0f)
        v = pv(lambda e: e.tensor_scalar(hst[1][:, :, 0], h03, col(SH_), None, ALU.mult), v_s2, v_z)
        vh = pv(lambda e: e.tensor_scalar(Hs, h0f, col(SH_), None, ALU.mult), v_s2)
        vn = pv(lambda e: e.memset(nc1, -0.5))
        v_h0 = pv(lambda e: e.tensor_tensor(hst[1][:, :, 2], c3(Hs), hst[1][:, :, 0], ALU.subtract), v, vh)
        pv(lambda e: e.tensor_scalar(bh, bh, col(C_SH), None, ALU.mult), v_cs)
        pv(lambda e: e.tensor_scalar(nc1, nc1, col(SH_), None, ALU.mult), vn)
        v_tr = pv(lambda e: e.tensor_scalar(col(C_TR), col(C_TN), 0.5, None, ALU.mult), v_tn)
        v_bn = pv(lambda e: e.tensor_copy(Tt[:, 8:12, 32:40],
                                          bh[:, 8:12].rearrange("p (c o) -> p c o", o=1).broadcast_to([P, KC, B])), v_tr)
        state = {"lo": v_h0, "H": v_bn, "zh": None}
        for k in range(8, 12):
            v_ihs[k] = next(ih_split)
        hh_split = split_row(W_HH, 12, col(SHH), lambda k: v_hhl[k // 6], v_s2)
        for k in range(12):
            act_now.pop(0)()
            if k < 8:
                next_gates(k + 4)
            v_hh_k = next(hh_split)
        v_hhs.append(v_hh_k)
        for _ in gates_0:
            pass
        v = prod(C_T0, PX1, PIH, 2.0 ** -28, v_bias[0])
        v_bias[1] = prod(C_GI1, C_T0, C_SH, 1.0, v)
        split_x(1)
        prod(C_IR, PR, PH, 2.0 ** -28, v_s2)
        prod(C_MIR, PR, PH, -(2.0 ** -28), v_s2)
        v = pv(lambda e: e.tensor_scalar(wr_h[:, 0], wr_raw, col(SR), None, ALU.mult), v_s2)
        pv(lambda e: e.tensor_copy(idh, idf), v_i)
        pv(lambda e: e.tensor_tensor(sel[0:16], idf[0:16, 0:8], idf[0:16, 8:16], ALU.add), v_i)
        v_small = pv(lambda e: e.scalar_tensor_tensor(out=wr_h[:, 1], in0=wr_raw, scalar=col(SR), in1=wr_h[:, 0],
                                                      op0=ALU.mult, op1=ALU.subtract), v)
        v_gil[0] = v_gil[1] = v_ev[10]
        state["placed"] = place_gates(0, v_ev[11])

        def bound_late(k):
            bound(24 + k, raw(D_MAX + 2 * k, 2 if k < 7 else 1), v_late[2 * k // 8])

        def bound_early(k):
            bound(32 + k, raw(W_D + SHIFT + 2 * k, 2 if k < 4 else 1), v_early[2 * k // 5],
                  v_early[min(2 * k + 1, EARLY - 1) // 5])

        def max_gu(k):
            v_maxs.append(rowmax(mx[:, k:k + 1], raw(W_GU + SHIFT + 2 * k, 2), v_gu[k // 4]))
            bounded(k)

        def load_gu(q):
            v_gu[q] = piece(wgu, W_GU + SHIFT + 8 * q, 8 * q, 8, f"ld_gu{q}", (v_xsums if q < 4 else v_sums)[-1])

        def load_early(q):
            v_early.append(piece(wd, W_D + SHIFT + 5 * q, 5 * q, (5, 4)[q], f"ld_e{q}", v_hm))

        loads = [(load_gu, 2), (load_gu, 3), (load_early, 0), (load_early, 1)]
        due = []

        def late_bounded():
            loads[0:0] = [(load_gu, 4), (load_gu, 5)]

        def follow_load(fn, q, t):
            if fn is load_gu:
                due.append((t, work, [(1150, lambda k=k: max_gu(k)) for k in range(4 * q, 4 * q + 4)]))
            elif q:
                due.append((t, act_work, [(950, lambda k=k: bound_early(k)) for k in range(5)]))

        def next_load(t):
            if loads and len(v_xsums) == 6:
                fn, q = loads.pop(0)
                fn(q)
                follow_load(fn, q, t + LOAD_STEPS)
            while due and due[0][0] <= t:
                due[0][1].extend(due[0][2])
                due.pop(0)

        for k in range(8):
            act_work.append((950, lambda k=k: bound_late(k)))
        act_work.append((0, late_bounded))
        for q in range(2):
            follow_load(load_gu, q, 1 + q)
        do_work(0.0, 0.0)
        do_work(1400.0, 0.0)
        for k in range(3, 6):
            sum_x(k)
        blocks += [input_gates(p) for p in range(1, NBLK)]
        for t in range(T):
            b = block_of[t]
            now[0] = t
            while t == BLOCKS[b][0] and b >= 2 and b - 2 not in v_hb_free:
                fill(2700.0)
                while act_now:
                    act_now.pop(0)()
                do_work(2500.0)
            v_mm = step_pe(t)
            while t == BLOCKS[1][0] and NBLK - 2 not in v_gi_piece:
                fill(2700.0)
                while act_now:
                    act_now.pop(0)()
                do_work(2500.0)
            fill(QUOTA if t < TB else (CATCH_UP if b - 1 not in begun else QUOTA_F))
            step(t, v_mm)
            next_load(t)
            do_work(WINDOW_0 if t < TB else (WINDOW_S if splits else WINDOW))
            if t + 1 == BLOCKS[b][0] + BLOCKS[b][1]:
                blocks.append(ffn(b, state["kept"]))
        now[0] = 2 * T
        while blocks or urgent or work or ew or late_dve or splits:
            fill(2700.0)
            while act_now:
                act_now.pop(0)()
            do_work(2500.0)

        block = ctx.enter_context(nc.Block())

        @block.sync
        def _(e):
            f.play("sp", e)
            for s in ("st_y", *(f"st_gi{k}" for k in range(NEV))):
                e.wait_ge(f.sems[s], f.count[s])

        @block.tensor
        def _(e):
            f.play("pe", e)

        @block.vector
        def _(e):
            f.play("dve", e)

        @block.scalar
        def _(e):
            f.play("act", e)


def kernel(x, cond_2048, L0_cond_W_ih, L0_cond_W_hh, L0_cond_b_ih, L0_cond_b_hh, L0_ffn_w_gate,
           L0_ffn_w_gate_up, L0_ffn_w_down, L0_ffn_w_sh_gate_up, L0_ffn_w_sh_down):
    import concourse.bacc as _bacc
    from concourse.bass_utils import run_bass_kernel_spmd as _run

    c = np.ascontiguousarray

    def rows(w):
        k, m = w.shape
        return np.asarray(w).reshape(k // 128, 128, m).transpose(1, 0, 2)

    arrays = {
        "x": c(np.asarray(x).transpose(2, 1, 0).reshape(4, 128, 8, 256).transpose(1, 2, 0, 3).reshape(128, 8192)),
        "h0": c(rows(np.asarray(cond_2048).T).reshape(128, 32)),
        "wih": c(rows(L0_cond_W_ih).reshape(128, 4, 3, 512).transpose(0, 2, 1, 3).reshape(128, 6144)),
        "whh": c(rows(L0_cond_W_hh).reshape(128, 6144)),
        "bih": c(np.asarray(L0_cond_b_ih).reshape(12, 128).T),
        "bhh": c(np.asarray(L0_cond_b_hh).reshape(12, 128).T),
        "wr": c(rows(L0_ffn_w_gate).reshape(128, 32)),
        "wgu": c(np.concatenate([rows(L0_ffn_w_sh_gate_up).reshape(128, 4, 4, 512)[:, :, [0, 2, 1, 3]].transpose(0, 2, 1, 3),
                                 np.asarray(L0_ffn_w_gate_up).reshape(8, 4, 128, 512).transpose(2, 0, 1, 3)],
                                axis=1).reshape(128, 24576)),
        "wd": c(np.concatenate([rows(L0_ffn_w_sh_down), rows(np.asarray(L0_ffn_w_down).reshape(2048, 512))],
                               axis=1).reshape(128, 12288)),
        "ident": np.eye(128, dtype=np.float32),
        "iota": c(np.broadcast_to(np.arange(8, dtype=np.float32), (128, 8))),
    }
    nc = _bacc.Bacc("TRN2", target_bir_lowering=False, num_devices=1)
    args = [nc.dram_tensor(n, a.shape, mybir.dt.from_np(a.dtype), kind="ExternalInput").ap()
            for n, a in arrays.items()]
    out = nc.dram_tensor("y", (128, 8192), F32, kind="ExternalOutput").ap()
    adaln_ffn(nc, *args, out)
    r = _run(nc, [arrays], core_ids=[0])
    got = r.results[0]["y"]
    return c(got.reshape(128, 8, 4, 32, 8).transpose(4, 1, 3, 2, 0).reshape(8, 256, 512))
```
